# Optimizing a Trainium2 kernel written in Bass

```python
import numpy as np
import jax
import jax.numpy as jnp

def _softmax(x, axis=-1):
    return jax.nn.softmax(x, axis=axis)

def _gelu(x):
    return jax.nn.gelu(x, approximate=True)

def _silu(x):
    return jax.nn.silu(x)

def _sigmoid(x):
    return jax.nn.sigmoid(x)

def _layernorm(x, axis=-1, eps=1e-05):
    m = jnp.mean(x, axis=axis, keepdims=True)
    v = jnp.var(x, axis=axis, keepdims=True)
    return (x - m) / jnp.sqrt(v + eps)

def _scatter_add(tgt, idx, src, axis=0):
    return tgt.at[idx].add(src)

def _segment_sum(src, seg, n):
    return jax.ops.segment_sum(src, seg, n)
kernel_name = 'mk_sandwich_d1_jaxref_r4_29ae3a'

def setup_inputs(seed: int=0):
    np.random.seed(seed)
    _w = jnp.asarray

    def _L0_attn_setup():
        import math
        import jax, jax.numpy as jnp
        import numpy as np
        D_MODEL = 256
        N_HEAD = 16
        HEAD_DIM = D_MODEL // N_HEAD
        B, T = (2, 512)

        def _layernorm(x, g, b, eps=1e-05):
            mu = jnp.mean(x, axis=-1, keepdims=True)
            var = jnp.mean(jnp.square(x - mu), axis=-1, keepdims=True)
            return (x - mu) * jax.lax.rsqrt(var + eps) * g + b

        def _l2norm(x, eps=1e-12):
            n = jnp.sqrt(jnp.sum(jnp.square(x), axis=-1, keepdims=True))
            return x / jnp.maximum(n, eps)

        def _rope(x, times):
            half = x.shape[-1] // 2
            freqs = jnp.exp(-jnp.arange(half, dtype=x.dtype) * (math.log(10000.0) / half))
            theta = times[:, None] * freqs[None, :]
            cos = jnp.cos(theta)[None, :, None, :]
            sin = jnp.sin(theta)[None, :, None, :]
            xr = x.reshape(*x.shape[:-1], half, 2)
            x1, x2 = (xr[..., 0], xr[..., 1])
            r1 = x1 * cos - x2 * sin
            r2 = x1 * sin + x2 * cos
            return jnp.stack([r1, r2], axis=-1).reshape(x.shape)
        key = jax.random.key(seed)
        ks = jax.random.split(key, 16)
        s = 0.02
        f32 = jnp.float32
        inp = {'x': jax.random.normal(ks[0], (B, T, D_MODEL), f32), 'Wq': jax.random.normal(ks[1], (D_MODEL, D_MODEL), f32) * s, 'Wk': jax.random.normal(ks[2], (D_MODEL, D_MODEL), f32) * s, 'Wv': jax.random.normal(ks[3], (D_MODEL, D_MODEL), f32) * s, 'gate_w': jax.random.normal(ks[4], (D_MODEL, D_MODEL), f32) * s, 'gate_b': jnp.zeros((D_MODEL,), f32), 'p_w': jax.random.normal(ks[5], (D_MODEL, D_MODEL), f32) * s, 'p_b': jnp.zeros((D_MODEL,), f32), 'out_w': jax.random.normal(ks[6], (D_MODEL, D_MODEL), f32) * s, 'out_b': jnp.zeros((D_MODEL,), f32), 'clock_w': jax.random.normal(ks[7], (D_MODEL, N_HEAD), f32) * s, 'clock_b': jnp.zeros((N_HEAD,), f32), 'ln1_g': jnp.ones((D_MODEL,), f32), 'ln1_b': jnp.zeros((D_MODEL,), f32), 'ln2_g': jnp.ones((D_MODEL,), f32), 'ln2_b': jnp.zeros((D_MODEL,), f32), 'mlp_w1': jax.random.normal(ks[8], (D_MODEL, 4 * D_MODEL), f32) * s, 'mlp_b1': jnp.zeros((4 * D_MODEL,), f32), 'mlp_w2': jax.random.normal(ks[9], (4 * D_MODEL, D_MODEL), f32) * s, 'mlp_b2': jnp.zeros((D_MODEL,), f32)}
        return inp
    _L0_attn_in = _L0_attn_setup()

    def _L0_ffn_setup():
        import jax, jax.numpy as jnp
        import numpy as np
        H = 256
        E = 32
        I = 128
        TOP_K = 6
        IS = 256
        NORM_MIN = 1e-12
        B, S = (2, 256)
        key = jax.random.key(seed)
        ks = jax.random.split(key, 8)
        sc = 0.02
        return {'hidden_states': jax.random.normal(ks[0], (B, S, H), jnp.float32), 'router_weight': jax.random.normal(ks[1], (E, H), jnp.float32) * sc, 'e_score_bias': jnp.zeros((E,), jnp.float32), 'gate_up_proj': jax.random.normal(ks[2], (E, 2 * I, H), jnp.float32) * sc, 'down_proj': jax.random.normal(ks[3], (E, H, I), jnp.float32) * sc, 'shared_gate_w': jax.random.normal(ks[4], (IS, H), jnp.float32) * sc, 'shared_up_w': jax.random.normal(ks[5], (IS, H), jnp.float32) * sc, 'shared_down_w': jax.random.normal(ks[6], (H, IS), jnp.float32) * sc}
    _L0_ffn_in = _L0_ffn_setup()
    _d = {'L0_attn_x': _L0_attn_in['x'], 'L0_attn_Wq': _L0_attn_in['Wq'], 'L0_attn_Wk': _L0_attn_in['Wk'], 'L0_attn_Wv': _L0_attn_in['Wv'], 'L0_attn_gate_w': _L0_attn_in['gate_w'], 'L0_attn_gate_b': _L0_attn_in['gate_b'], 'L0_attn_p_w': _L0_attn_in['p_w'], 'L0_attn_p_b': _L0_attn_in['p_b'], 'L0_attn_out_w': _L0_attn_in['out_w'], 'L0_attn_out_b': _L0_attn_in['out_b'], 'L0_attn_clock_w': _L0_attn_in['clock_w'], 'L0_attn_clock_b': _L0_attn_in['clock_b'], 'L0_attn_ln1_g': _L0_attn_in['ln1_g'], 'L0_attn_ln1_b': _L0_attn_in['ln1_b'], 'L0_attn_ln2_g': _L0_attn_in['ln2_g'], 'L0_attn_ln2_b': _L0_attn_in['ln2_b'], 'L0_attn_mlp_w1': _L0_attn_in['mlp_w1'], 'L0_attn_mlp_b1': _L0_attn_in['mlp_b1'], 'L0_attn_mlp_w2': _L0_attn_in['mlp_w2'], 'L0_attn_mlp_b2': _L0_attn_in['mlp_b2'], 'L0_ffn_router_weight': _L0_ffn_in['router_weight'], 'L0_ffn_e_score_bias': _L0_ffn_in['e_score_bias'], 'L0_ffn_gate_up_proj': _L0_ffn_in['gate_up_proj'], 'L0_ffn_down_proj': _L0_ffn_in['down_proj'], 'L0_ffn_shared_gate_w': _L0_ffn_in['shared_gate_w'], 'L0_ffn_shared_up_w': _L0_ffn_in['shared_up_w'], 'L0_ffn_shared_down_w': _L0_ffn_in['shared_down_w']}
    _x0 = _d['L0_attn_x']
    _d['L0_attn_x'] = jax.random.normal(jax.random.fold_in(jax.random.key(seed), 1), (1, 4096, 256), dtype=_x0.dtype)
    del _x0
    return _d

def reference(L0_attn_x, L0_attn_Wq, L0_attn_Wk, L0_attn_Wv, L0_attn_gate_w, L0_attn_gate_b, L0_attn_p_w, L0_attn_p_b, L0_attn_out_w, L0_attn_out_b, L0_attn_clock_w, L0_attn_clock_b, L0_attn_ln1_g, L0_attn_ln1_b, L0_attn_ln2_g, L0_attn_ln2_b, L0_attn_mlp_w1, L0_attn_mlp_b1, L0_attn_mlp_w2, L0_attn_mlp_b2, L0_ffn_router_weight, L0_ffn_e_score_bias, L0_ffn_gate_up_proj, L0_ffn_down_proj, L0_ffn_shared_gate_w, L0_ffn_shared_up_w, L0_ffn_shared_down_w):

    def _L0_attn_ref(x, Wq, Wk, Wv, gate_w, gate_b, p_w, p_b, out_w, out_b, clock_w, clock_b, ln1_g, ln1_b, ln2_g, ln2_b, mlp_w1, mlp_b1, mlp_w2, mlp_b2):
        import math
        import jax, jax.numpy as jnp
        import numpy as np
        D_MODEL = 256
        N_HEAD = 16
        HEAD_DIM = D_MODEL // N_HEAD
        B, T = (2, 512)

        def _layernorm(x, g, b, eps=1e-05):
            mu = jnp.mean(x, axis=-1, keepdims=True)
            var = jnp.mean(jnp.square(x - mu), axis=-1, keepdims=True)
            return (x - mu) * jax.lax.rsqrt(var + eps) * g + b

        def _l2norm(x, eps=1e-12):
            n = jnp.sqrt(jnp.sum(jnp.square(x), axis=-1, keepdims=True))
            return x / jnp.maximum(n, eps)

        def _rope(x, times):
            half = x.shape[-1] // 2
            freqs = jnp.exp(-jnp.arange(half, dtype=x.dtype) * (math.log(10000.0) / half))
            theta = times[:, None] * freqs[None, :]
            cos = jnp.cos(theta)[None, :, None, :]
            sin = jnp.sin(theta)[None, :, None, :]
            xr = x.reshape(*x.shape[:-1], half, 2)
            x1, x2 = (xr[..., 0], xr[..., 1])
            r1 = x1 * cos - x2 * sin
            r2 = x1 * sin + x2 * cos
            return jnp.stack([r1, r2], axis=-1).reshape(x.shape)
        Bx, Tx, D = x.shape
        H, Dh = (N_HEAD, HEAD_DIM)
        residual = x
        xn = _layernorm(x, ln1_g, ln1_b)
        times = jnp.arange(Tx, dtype=x.dtype)
        q = _l2norm((xn @ Wq).reshape(Bx, Tx, H, Dh))
        k = _l2norm((xn @ Wk).reshape(Bx, Tx, H, Dh))
        v = (xn @ Wv).reshape(Bx, Tx, H, Dh)
        clock = jax.nn.softplus(xn @ clock_w + clock_b).reshape(Bx, Tx, H, 1)
        q = _rope(q, times)
        k = _rope(k, times)
        gj = -jax.nn.softplus(xn @ gate_w + gate_b).reshape(Bx, Tx, H, Dh)
        gcp = jnp.exp(jnp.clip(jnp.cumsum(gj, axis=1), -60.0, 50.0))
        q = q * gcp
        k = k / (gcp + 1e-08)
        p = (xn @ p_w + p_b).reshape(Bx, Tx, H, Dh)
        p_max = jnp.max(p, axis=1, keepdims=True)
        p_exp = jnp.exp(p - p_max) * clock
        p_cs = jnp.cumsum(p_exp, axis=1)
        q = q / (p_cs + 1e-08)
        k = k * p_exp
        scores = jnp.einsum('bqhd,bkhd->bhqk', q, k) / math.sqrt(Dh)
        mask = jnp.tril(jnp.ones((Tx, Tx), dtype=bool))
        scores = jnp.where(mask[None, None], scores, -jnp.inf)
        attn = jax.nn.softmax(scores, axis=-1)
        out = jnp.einsum('bhqk,bkhd->bqhd', attn, v).reshape(Bx, Tx, D)
        out = out @ out_w + out_b
        x1 = out + residual
        h = _layernorm(x1, ln2_g, ln2_b)
        h = jax.nn.gelu(h @ mlp_w1 + mlp_b1, approximate=False) @ mlp_w2 + mlp_b2
        return x1 + h

    def _L0_ffn_ref(hidden_states, router_weight, e_score_bias, gate_up_proj, down_proj, shared_gate_w, shared_up_w, shared_down_w):
        import jax, jax.numpy as jnp
        import numpy as np
        H = 256
        E = 32
        I = 128
        TOP_K = 6
        IS = 256
        NORM_MIN = 1e-12
        B, S = (2, 256)
        b, s, h = hidden_states.shape
        x = hidden_states.reshape(-1, h)
        T = x.shape[0]
        shared_out = jax.nn.silu(x @ shared_gate_w.T) * (x @ shared_up_w.T) @ shared_down_w.T
        xf = x.astype(jnp.float32)
        router_logits = xf @ router_weight.T
        routing_weights = jax.nn.softmax(router_logits, axis=-1)
        corrected = routing_weights + e_score_bias
        _, top_idx = jax.lax.top_k(corrected, TOP_K)
        top_w = jnp.take_along_axis(routing_weights, top_idx, axis=-1)
        top_w = top_w / jnp.clip(top_w.sum(axis=-1, keepdims=True), NORM_MIN)
        top_w = top_w.astype(x.dtype)
        combine = jnp.zeros((T, E), x.dtype).at[jnp.arange(T)[:, None], top_idx].add(top_w)
        gu = jnp.einsum('th,eih->tei', x, gate_up_proj)
        gate, up = jnp.split(gu, 2, axis=-1)
        hmid = jax.nn.silu(gate) * up
        y = jnp.einsum('tei,ehi->teh', hmid, down_proj)
        out = jnp.einsum('teh,te->th', y, combine) + shared_out
        return out.reshape(b, s, h)
    x = L0_attn_x
    x = x + _layernorm(_L0_attn_ref(_layernorm(x, axis=-1), L0_attn_Wq, L0_attn_Wk, L0_attn_Wv, L0_attn_gate_w, L0_attn_gate_b, L0_attn_p_w, L0_attn_p_b, L0_attn_out_w, L0_attn_out_b, L0_attn_clock_w, L0_attn_clock_b, L0_attn_ln1_g, L0_attn_ln1_b, L0_attn_ln2_g, L0_attn_ln2_b, L0_attn_mlp_w1, L0_attn_mlp_b1, L0_attn_mlp_w2, L0_attn_mlp_b2), axis=-1)
    x = x + _layernorm(_L0_ffn_ref(_layernorm(x, axis=-1), L0_ffn_router_weight, L0_ffn_e_score_bias, L0_ffn_gate_up_proj, L0_ffn_down_proj, L0_ffn_shared_gate_w, L0_ffn_shared_up_w, L0_ffn_shared_down_w), axis=-1)
    return x

_drawn_inputs = setup_inputs


def setup_inputs(seed=0):
    import zlib

    import numpy as np

    out = dict(_drawn_inputs(seed))
    spreads = {'L0_attn_gate_b': (0.0, 2.0),
     'L0_attn_p_b': (0.0, 2.0),
     'L0_attn_out_b': (0.0, 0.552),
     'L0_attn_clock_b': (0.0, 2.0),
     'L0_attn_ln1_g': (1.0, 0.6),
     'L0_attn_ln1_b': (0.0, 0.8),
     'L0_attn_ln2_g': (1.0, 0.6),
     'L0_attn_ln2_b': (0.0, 2.0),
     'L0_attn_mlp_b1': (0.0, 1.185),
     'L0_attn_mlp_b2': (0.0, 0.478),
     'L0_ffn_e_score_bias': (0.0, 0.1)}
    factors = {'L0_attn_Wq': 200.0,
     'L0_attn_Wk': 200.0,
     'L0_attn_Wv': 8.0,
     'L0_attn_gate_w': 200.0,
     'L0_attn_p_w': 200.0,
     'L0_attn_out_w': 8.0,
     'L0_attn_clock_w': 200.0}
    for name, (base, spread) in spreads.items():
        noise = np.random.default_rng([zlib.crc32(name.encode()), seed]).standard_normal(out[name].shape)
        drawn = base * np.exp(spread * noise) if base else spread * noise
        out[name] = jnp.asarray(drawn.astype(out[name].dtype))
    for name, factor in factors.items():
        out[name] = (out[name] * factor).astype(out[name].dtype)
    return out
```

```python
from contextlib import ExitStack

import concourse.bass as bass
from concourse import mybir

ALU = mybir.AluOpType
ACT = mybir.ActivationFunctionType
AX = mybir.AxisListType
F32 = mybir.dt.float32
F32R = mybir.dt.float32r
BF16 = mybir.dt.bfloat16
U32 = mybir.dt.uint32

P = 128
T = 4096
D = 256
H = 16
DH = D // H
KT = D // P
CH = 512
NCH = T // CH
TPC = CH // P
NT = T // P
FF = 4 * D
FT = FF // P
NE = 32
NI = 128
TOPK = 6
EPS = 1e-5
QSCALE = 2.0 ** 40
BIG = -3e38
FILLER = NE + 2
FIXED = 2 * NCH
ROUND = 4
PARTS = 3
NPROD = 6
Q_PARTS = (0, 0, 1, 1, 0, 2)
K_PARTS = (0, 1, 0, 1, 2, 0)
SROWS = NPROD * DH


class Steps:

    def __init__(self, engine, sem, base=0):
        self.engine, self.sem, self.base, self.count = engine, sem, base, 0

    def step(self, ins):
        self.count += 1
        return ins.then_inc(self.sem, 1)

    def done(self):
        self.engine.wait_ge(self.sem, self.base + self.count)


def by_part(ap):
    return ap.rearrange("(t p) n -> p t n", p=P)


def project_phase(nc, a, keep):
    DVE_STEPS = 4 + 3 * TPC + 5 * KT
    with ExitStack() as ctx:
        def sb(name, shape, dt=F32):
            return ctx.enter_context(nc.sbuf_tensor(name, shape, dt))

        def psum(name, shape):
            return ctx.enter_context(nc.psum_tensor(name, shape, F32))

        def sem(name):
            return ctx.enter_context(nc.semaphore(name))

        wqk = sb("wqk", [P, KT, 2 * D])
        wvc = sb("wvc", [P, KT, D + H])
        wgp = sb("wgp", [P, KT, 2 * D])
        g1 = sb("g1", [P, KT])
        b1 = sb("b1", [P, KT])
        gpb = sb("gpb", [P, 2 * KT])
        clockb = sb("clockb", [P, H])
        rot_c = sb("rot_c", [P, NT, DH])
        rot_s = sb("rot_s", [P, NT, DH])
        neghalf = sb("neghalf", [P, TPC])
        ones = sb("ones_row", [P, CH])
        xin = sb("xin", [P, 2, TPC, D])
        x0 = sb("x0", [P, TPC, D])
        xn = sb("xn", [P, TPC, D])
        stats = sb("stats", [P, TPC, 6])
        mv = sb("mv", [P, TPC, 2])
        veps = sb("veps", [P, TPC])
        rstd = sb("rstd", [P, TPC])
        xnt = sb("xnt", [P, KT, CH])
        sq = sb("sq", [P, 2, 2 * D])
        ssq = sb("ssq", [P, 2 * H])
        nrm = sb("nrm", [P, 2 * H])
        rnrm = sb("rnrm", [P, 2 * H])
        qkn = sb("qkn", [P, 2 * D])
        rc = sb("rc", [P, 2 * D])
        rs = sb("rs", [P, 2 * D])
        qkr = sb("qkr", [P, 2, 2 * D])
        qkt = sb("qkt", [P, 2 * KT, CH])
        gx = sb("gx", [P, CH])
        ga = sb("ga", [P, CH])
        ge = sb("ge", [P, CH])
        gl = sb("gl", [P, CH])
        gd = sb("gd", [P, CH])
        gc = sb("gc", [P, CH])
        gsp = sb("gsp", [P, CH])
        gsum = sb("gsum", [P, CH])
        spare = sb("spare", [P, 1])
        epst = sb("epst", [P, TPC])
        carry = sb("carry", [P, KT])
        gclip = sb("gclip", [P, CH])

        ps_xt = psum("ps_xt", [P, KT, CH])
        ps_qk = psum("ps_qk", [P, 2, 2 * D])
        ps_vc = psum("ps_vc", [P, CH])
        ps_gp = psum("ps_gp", [P, CH])
        ps_rt = psum("ps_rt", [P, 2, 2 * KT, P])

        s_const = sem("p1_const")
        s_x = sem("p1_x")
        s_dve = sem("p1_dve")
        s_var = sem("p1_var")
        s_veps = sem("p1_veps")
        s_rstd = sem("p1_rstd")
        s_x0 = sem("p1_x0")
        s_x0out = sem("p1_x0out")
        s_xn = sem("p1_xn")
        s_xt = sem("p1_xt")
        s_xnt = sem("p1_xnt")
        s_qk = sem("p1_qk")
        s_vc = sem("p1_vc")
        s_v = sem("p1_v")
        s_sq = sem("p1_sq")
        s_ssq = sem("p1_ssq")
        s_nrm = sem("p1_nrm")
        s_qkn = sem("p1_qkn")
        s_swap = sem("p1_swap")
        s_qkr = sem("p1_qkr")
        s_rt = sem("p1_rt")
        s_qkt = sem("p1_qkt")
        s_qktout = sem("p1_qktout")
        s_gp = sem("p1_gp")
        s_gx = sem("p1_gx")
        s_act = sem("p1_act")
        s_ln = sem("p1_ln")
        s_gclip = sem("p1_gclip")
        s_gexp = sem("p1_gexp")
        s_pt = sem("p1_pt")
        s_clock = sem("p1_clock")
        NLOADS = 13

        x_dram = a["x"].rearrange("a (c t p) d -> c (a p) t d", t=TPC, p=P)
        x0_dram = a["x0"].rearrange("(c t p) d -> c p t d", t=TPC, p=P)
        qkt_dram = a["qkt"].rearrange("(m p) (c n) -> c p m n", p=P, n=CH)

        block = ctx.enter_context(nc.Block())

        @block.sync
        def _(sp):
            sp.dma_start(wqk[:, :, 0:D], by_part(a["wq"])).then_inc(s_const, 16)
            sp.dma_start(wqk[:, :, D:], by_part(a["wk"])).then_inc(s_const, 16)
            sp.dma_start(wvc[:, :, 0:D], by_part(a["wv"])).then_inc(s_const, 16)
            sp.dma_start(wvc[:, :, D:], by_part(a["clock_w"])).then_inc(s_const, 16)
            sp.dma_start(wgp[:, :, 0:D], by_part(a["gate_w"])).then_inc(s_const, 16)
            sp.dma_start(wgp[:, :, D:], by_part(a["p_w"])).then_inc(s_const, 16)
            sp.dma_start(g1[:, :], a["ln1_g"]).then_inc(s_const, 16)
            sp.dma_start(b1[:, :], a["ln1_b"]).then_inc(s_const, 16)
            sp.dma_start(gpb[:, 0:KT], a["gate_b"]).then_inc(s_const, 16)
            sp.dma_start(gpb[:, KT:], a["p_b"]).then_inc(s_const, 16)
            sp.dma_start(clockb[:, :], a["clock_b"]).then_inc(s_const, 16)
            sp.dma_start(rot_c[:, :, :], by_part(a["rot_c"])).then_inc(s_const, 16)
            sp.dma_start(rot_s[:, :, :], by_part(a["rot_s"])).then_inc(s_const, 16)
            with sp.Fori(0, NCH // 2) as pair:
                for b in range(2):
                    c = pair * 2 + b
                    sp.wait_ge(s_x0, c)
                    sp.dma_start(xin[:, b, :, :], x_dram[bass.ds(c, 1)].rearrange("a p t d -> p (a t) d")).then_inc(s_x, 16)
                    sp.wait_ge(s_x0, c + 1)
                    sp.dma_start(x0_dram[bass.ds(c, 1)].rearrange("a p t d -> p (a t) d"), x0[:, :, :]).then_inc(s_x0out, 16)
                    sp.wait_ge(s_qkt, TPC * (c + 1))
                    sp.dma_start(qkt_dram[bass.ds(c, 1)].rearrange("a p m n -> p (a m) n"), qkt[:, :, :]).then_inc(s_qktout, 16)
            sp.wait_ge(s_x0out, 16 * NCH)
            sp.wait_ge(s_qktout, 16 * NCH)

        @block.vector
        def _(dve):
            v = nc.vector
            v.memset(neghalf[:, :], -0.5).then_inc(s_dve, 1)
            v.memset(ones[:, :], 1.0).then_inc(s_dve, 1)
            v.memset(epst[:, :], EPS).then_inc(s_dve, 1)
            v.memset(carry[:, :], 0.0).then_inc(s_dve, 1)
            dve.wait_ge(s_const, 16 * NLOADS)

            def layernorm(st, c, src, out, nth, out_sem):
                for t in range(TPC):
                    ins = v.bn_stats(stats[:, t, :], src[:, t, :])
                st.step(ins)
                st.done()
                st.step(v.memset(spare[:, :], 0.0))
                for t in range(TPC):
                    ins = v.bn_aggr(mv[:, t, :], stats[:, t, :])
                ins.then_inc(s_var, 1)
                dve.wait_ge(s_rstd, 2 * c + nth)
                for t in range(TPC):
                    ins = v.tensor_scalar(out[:, t, :], src[:, t, :], mv[:, t, 0:1], rstd[:, t:t + 1],
                                          ALU.subtract, ALU.mult)
                ins.then_inc(out_sem, 1)

            with dve.Fori(0, NCH // 2) as pair:
                for b in range(2):
                    c = pair * 2 + b
                    st = Steps(dve, s_dve, c * DVE_STEPS + 4)
                    dve.wait_ge(s_x, 16 * (c + 1))
                    dve.wait_ge(s_x0out, 16 * c)
                    layernorm(st, c, xin[:, b], x0, 1, s_x0)
                    dve.wait_ge(s_x0, c + 1)
                    dve.wait_ge(s_xt, c)
                    layernorm(st, c, x0, xn, 2, s_xn)

                    for t in range(TPC):
                        n = c * TPC + t
                        dve.wait_ge(s_v, n + 1)
                        v.tensor_tensor(keep["clk"][:, bass.ds(n, 1), :].rearrange("p a h -> p (a h)"),
                                        ps_vc[:, D:D + H], clockb[:, :], ALU.add).then_inc(s_clock, 1)
                        dve.wait_ge(s_sq, n + 1)
                        v.tensor_reduce(ssq[:, :], sq[:, t % 2, :].rearrange("p (h d) -> p h d", d=DH),
                                        AX.X, ALU.add).then_inc(s_ssq, 1)
                        dve.wait_ge(s_nrm, n + 1)
                        st.step(v.tensor_scalar(nrm[:, :], nrm[:, :], 1e-12, None, ALU.max))
                        st.done()
                        st.step(v.reciprocal(rnrm[:, :], nrm[:, :]))
                        st.done()
                        dve.wait_ge(s_swap, n)
                        v.tensor_tensor(qkn[:, :].rearrange("p (h d) -> p h d", d=DH),
                                        ps_qk[:, t % 2, :].rearrange("p (h d) -> p h d", d=DH),
                                        rnrm[:, :].rearrange("p (h a) -> p h a", a=1).to_broadcast([P, 2 * H, DH]),
                                        ALU.mult).then_inc(s_qkn, 1)
                        dve.wait_ge(s_qkn, n + 1)
                        st.step(v.tensor_tensor(rc[:, :].rearrange("p (h d) -> p h d", d=DH),
                                                qkn[:, :].rearrange("p (h d) -> p h d", d=DH),
                                                rot_c[:, bass.ds(n, 1), :].to_broadcast([P, 2 * H, DH]), ALU.mult))
                        st.done()
                        dve.wait_ge(s_swap, n + 1)
                        if t >= 2:
                            dve.wait_ge(s_rt, n - 1)
                        else:
                            dve.wait_ge(s_rt, c * TPC)
                        v.tensor_tensor(qkr[:, t % 2, :], rc[:, :], rs[:, :], ALU.add).then_inc(s_qkr, 1)

                    for m in range(KT):
                        dve.wait_ge(s_ln, KT * c + m + 1)
                        st.step(v.tensor_scalar(gd[:, :], ge[:, :], 1.0, -1.0, ALU.add, ALU.add))
                        st.done()
                        st.step(v.tensor_tensor(gc[:, :], ge[:, :], gd[:, :], ALU.subtract))
                        st.done()
                        st.step(v.tensor_tensor(gc[:, :], gc[:, :], gl[:, :], ALU.add))
                        st.done()
                        st.step(v.scalar_tensor_tensor(out=gsp[:, :], in0=gx[:, :], scalar=0.0, in1=gc[:, :],
                                                       op0=ALU.max, op1=ALU.add))
                        st.done()
                        st.step(v.tensor_tensor_scan(gsum[:, :], ones[:, :], gsp[:, :], carry[:, m:m + 1],
                                                     ALU.mult, ALU.subtract))
                        st.done()
                        dve.wait_ge(s_gexp, KT * c + m)
                        v.tensor_copy(carry[:, m:m + 1], gsum[:, CH - 1:CH])
                        v.tensor_scalar(gclip[:, :], gsum[:, :], -60.0, 50.0, ALU.max, ALU.min).then_inc(s_gclip, 1)

        @block.gpsimd
        def _(pool):
            g = nc.gpsimd
            pool.wait_ge(s_dve, 4)
            pool.wait_ge(s_const, 16 * NLOADS)
            with pool.Fori(0, NCH) as c:
                for nth in range(2):
                    pool.wait_ge(s_var, 2 * c + nth + 1)
                    g.tensor_tensor(veps[:, :], mv[:, :, 1], epst[:, :], ALU.add).then_inc(s_veps, 1)
                    pool.wait_ge(s_veps, 2 * c + nth + 1)
                    g.tensor_tensor(rstd[:, :], veps[:, :], neghalf[:, :], ALU.pow).then_inc(s_rstd, 1)
                for t in range(TPC):
                    n = c * TPC + t
                    pool.wait_ge(s_qkn, n + 1)
                    pool.wait_ge(s_qkr, n)
                    src = qkn[:, :].rearrange("p (h d two) -> p h d two", d=DH // 2, two=2)
                    dst = rs[:, :].rearrange("p (h d two) -> p h d two", d=DH // 2, two=2)
                    rot = rot_s[:, bass.ds(n, 1), :].rearrange("p a (d two) -> p a d two", two=2)
                    for i in range(2):
                        ins = g.tensor_tensor(dst[:, :, :, i], src[:, :, :, 1 - i],
                                              rot[:, :, :, i].to_broadcast([P, 2 * H, DH // 2]), ALU.mult)
                    ins.then_inc(s_swap, 1)

        @block.scalar
        def _(act):
            s = nc.scalar
            act.wait_ge(s_const, 16 * NLOADS)
            with act.Fori(0, NCH) as c:
                act.wait_ge(s_xt, c + 1)
                act.wait_ge(s_gp, 2 * KT * c)
                for m in range(KT):
                    ins = s.activation(xnt[:, m, :], ps_xt[:, m, :], ACT.Identity, bias=b1[:, m:m + 1],
                                       scale=g1[:, m:m + 1])
                ins.then_inc(s_xnt, 1)
                for t in range(TPC):
                    n = c * TPC + t
                    act.wait_ge(s_qk, n + 1)
                    if t >= 2:
                        act.wait_ge(s_ssq, n - 1)
                    else:
                        act.wait_ge(s_ssq, c * TPC)
                    s.activation(sq[:, t % 2, :], ps_qk[:, t % 2, :], ACT.Square).then_inc(s_sq, 1)
                    act.wait_ge(s_vc, n + 1)
                    s.activation(keep["v"][:, bass.ds(n, 1), :].rearrange("p a d -> p (a d)"), ps_vc[:, 0:D],
                                 ACT.Copy).then_inc(s_v, 1)
                    act.wait_ge(s_ssq, n + 1)
                    act.wait_ge(s_qkn, n)
                    s.activation(nrm[:, :], ssq[:, :], ACT.Sqrt).then_inc(s_nrm, 1)
                    if t == 0:
                        act.wait_ge(s_qktout, 16 * c)
                    act.wait_ge(s_rt, n + 1)
                    s.activation(qkt[:, :, t * P:(t + 1) * P], ps_rt[:, t % 2, :, :], ACT.Copy).then_inc(s_qkt, 1)
                for m in range(KT):
                    act.wait_ge(s_gp, 2 * KT * c + m + 1)
                    s.activation(keep["pt"][:, m, bass.ds(c * CH, CH)], ps_gp[:, :], ACT.Identity,
                                 bias=gpb[:, KT + m:KT + m + 1]).then_inc(s_pt, 1)
                for m in range(KT):
                    act.wait_ge(s_gp, 2 * KT * c + KT + m + 1)
                    act.wait_ge(s_gclip, KT * c + m)
                    s.activation(gx[:, :], ps_gp[:, :], ACT.Identity, bias=gpb[:, m:m + 1]).then_inc(s_gx, 1)
                    act.wait_ge(s_gx, KT * c + m + 1)
                    s.activation(ga[:, :], gx[:, :], ACT.Abs).then_inc(s_act, 1)
                    act.wait_ge(s_act, 2 * (KT * c + m) + 1)
                    s.activation(ge[:, :], ga[:, :], ACT.Exp, scale=-1.0).then_inc(s_act, 1)
                    act.wait_ge(s_act, 2 * (KT * c + m) + 2)
                    s.activation(gl[:, :], ge[:, :], ACT.Ln, bias=1.0).then_inc(s_ln, 1)
                    act.wait_ge(s_gclip, KT * c + m + 1)
                    s.activation(keep["gt"][:, m, bass.ds(c * CH, CH)], gclip[:, :], ACT.Exp).then_inc(s_gexp, 1)

        @block.tensor
        def _(pe):
            m_ = nc.tensor
            pe.wait_ge(s_const, 16 * NLOADS)
            with pe.Fori(0, NCH) as c:
                pe.wait_ge(s_xn, c + 1)
                pe.wait_ge(s_xnt, c)
                for t in range(TPC):
                    for m in range(KT):
                        ins = m_.transpose(ps_xt[:, m, t * P:(t + 1) * P], xn[:, t, m * P:(m + 1) * P],
                                           keep["ident"][:, :])
                ins.then_inc(s_xt, 1)
                pe.wait_ge(s_xnt, c + 1)

                def rotate_back(t):
                    n = c * TPC + t
                    pe.wait_ge(s_qkr, n + 1)
                    if t >= 2:
                        pe.wait_ge(s_qkt, n - 1)
                    else:
                        pe.wait_ge(s_qkt, c * TPC)
                    for m in range(2 * KT):
                        ins = m_.transpose(ps_rt[:, t % 2, m, :], qkr[:, t % 2, m * P:(m + 1) * P],
                                           keep["ident"][:, :])
                    ins.then_inc(s_rt, 1)

                for t in range(TPC):
                    n = c * TPC + t
                    tok = slice(t * P, (t + 1) * P)
                    if t >= 2:
                        pe.wait_ge(s_qkn, n - 1)
                    else:
                        pe.wait_ge(s_qkn, c * TPC)
                    for k in range(KT):
                        ins = m_.matmul(ps_qk[:, t % 2, :], xnt[:, k, tok], wqk[:, k, :], start=(k == 0), stop=(k == KT - 1))
                    ins.then_inc(s_qk, 1)
                    pe.wait_ge(s_v, n)
                    pe.wait_ge(s_clock, n)
                    for k in range(KT):
                        ins = m_.matmul(ps_vc[:, 0:D + H], xnt[:, k, tok], wvc[:, k, :], start=(k == 0), stop=(k == KT - 1))
                    ins.then_inc(s_vc, 1)
                    if t >= 1:
                        rotate_back(t - 1)
                rotate_back(TPC - 1)
                for m in range(2 * KT):
                    if m <= KT:
                        pe.wait_ge(s_pt, KT * c + m)
                    if m == 0:
                        pe.wait_ge(s_gx, KT * c)
                    if m > KT:
                        pe.wait_ge(s_gx, KT * c + m - KT)
                    col = (KT + m if m < KT else m - KT) * P
                    for k in range(KT):
                        ins = m_.matmul(ps_gp[:, :], wgp[:, k, col:col + P], xnt[:, k, :], start=(k == 0), stop=(k == KT - 1))
                    ins.then_inc(s_gp, 1)


def stack_phase(nc, a, keep):
    CLOCK_STEPS = 5
    with ExitStack() as ctx:
        def sb(name, shape, dt=F32):
            return ctx.enter_context(nc.sbuf_tensor(name, shape, dt))

        def sem(name):
            return ctx.enter_context(nc.semaphore(name))

        qk = sb("qk_in", [P, 2, 2, CH])
        cabs = sb("cabs", [P, NT, H])
        cexp = sb("cexp", [P, NT, H])
        cln = sb("cln", [P, NT, H])
        clow = sb("clow", [P, NT, H])
        stage = sb("stage", [P, 2, TPC, P])
        npmax = sb("npmax", [P, KT])
        pe_x = sb("pe_x", [P, 2, CH])
        pexp = sb("pexp", [P, 2, CH])
        pcs = sb("pcs", [P, CH])
        pcarry = sb("pcarry", [P, KT])
        onesr = sb("onesr", [P, CH])
        pcs8 = sb("pcs8", [P, 2, CH])
        ge_pcs = sb("ge_pcs", [P, CH])
        rec = sb("rec", [P, 2, CH])
        num = sb("num", [P, CH])
        rge = sb("rge", [P, CH])
        ge8 = sb("ge8", [P, CH])
        fac = sb("fac", [P, 2, CH])
        full = sb("full", [P, 2, CH])
        rest = sb("rest", [P, 2, CH])
        parts = sb("parts", [P, 2, 2, PARTS, CH], BF16)
        ps_ct = ctx.enter_context(nc.psum_tensor("ps_ct", [P, 2, CH], F32))

        s_in = sem("p2_in")
        s_cabs = sem("p2_cabs")
        s_dve = sem("p2_dve")
        s_clk = sem("p2_clk")
        s_stage = sem("p2_stage")
        s_ct = sem("p2_ct")
        s_max = sem("p2_max")
        s_pexp = sem("p2_pexp")
        s_scan = sem("p2_scan")
        s_carry = sem("p2_carry")
        s_prod = sem("p2_prod")
        s_div = sem("p2_div")
        s_num = sem("p2_num")
        s_rec = sem("p2_rec")
        s_fac = sem("p2_fac")
        s_pe = sem("p2_pe")
        s_hi = sem("p2_hi")
        s_rest = sem("p2_rest")
        s_mid = sem("p2_mid")
        s_lo = sem("p2_lo")
        s_full = sem("p2_full")
        s_out = [sem(f"p2_out{b}") for b in range(2)]

        qkt_dram = a["qkt"].rearrange("(w m p) (c n) -> m c p w n", w=2, p=P, n=CH)
        parts_dram = a["parts"].rearrange("w r (m p) (c n) -> m c p (w r) n", p=P, n=CH)
        pt, gt, clk = keep["pt"], keep["gt"], keep["clk"]
        block = ctx.enter_context(nc.Block())

        def units(engine):
            for m in range(KT):
                with engine.Fori(0, NCH // 2) as pair:
                    for b in range(2):
                        yield m, pair * 2 + b, b, pair * 2 + (m * NCH + b)

        def in_turn(engine, both):
            for m in range(KT):
                def unit(c, b):
                    return m, c, b, c + m * NCH

                both(unit(0, 0), None)
                with engine.Fori(0, NCH // 2 - 1) as pair:
                    for b in (1, 0):
                        both(unit(pair * 2 + (2 - b), b), unit(pair * 2 + (1 - b), 1 - b))
                both(unit(NCH - 1, 1), unit(NCH - 2, 0))
                both(None, unit(NCH - 1, 1))

        def staggered(engine, first, second):
            def both(new, old):
                if new:
                    first(*new)
                if old:
                    second(*old)

            in_turn(engine, both)

        @block.sync
        def _(sp):
            for m, c, b, u in units(sp):
                sp.wait_ge(s_full, u)
                sp.dma_start(qk[:, b, :, :], qkt_dram[m, bass.ds(c, 1)].rearrange("a p w n -> p (a w) n")).then_inc(s_in, 16)
            for b in range(2):
                sp.wait_ge(s_out[b], 16 * KT * NCH // 2)

        @block.scalar
        def _(act):
            s = nc.scalar
            s.activation(cabs[:, :, :], clk[:, :, :], ACT.Abs).then_inc(s_cabs, 1)
            act.wait_ge(s_cabs, 1)
            s.activation(cexp[:, :, :], cabs[:, :, :], ACT.Exp, scale=-1.0).then_inc(s_cabs, 1)
            act.wait_ge(s_cabs, 2)
            s.activation(cln[:, :, :], cexp[:, :, :], ACT.Ln, bias=1.0).then_inc(s_cabs, 1)
            act.wait_ge(s_max, 1)

            def first(m, c, b, u):
                act.wait_ge(s_pe, u)
                s.activation(pe_x[:, b, :], pt[:, m, bass.ds(c * CH, CH)], ACT.Exp,
                             bias=npmax[:, m:m + 1]).then_inc(s_pexp, 1)

            def second(m, c, b, u):
                act.wait_ge(s_out[b], (16 // 2) * (u - b))
                act.wait_ge(s_full, u + 1)
                s.activation(parts[:, b, :, 0, :], full[:, :, :], ACT.Copy).then_inc(s_hi, 1)
                act.wait_ge(s_rest, u + 1)
                s.activation(parts[:, b, :, 1, :], rest[:, :, :], ACT.Copy).then_inc(s_mid, 1)
                act.wait_ge(s_lo, u + 1)
                act.dma_start(parts_dram[m, bass.ds(c, 1)].rearrange("a p r n -> p (a r) n"),
                              parts[:, b].rearrange("p w r n -> p (w r) n")).then_inc(s_out[b], 16)

            staggered(act, first, second)

        @block.gpsimd
        def _(pool):
            g = nc.gpsimd
            pool.wait_ge(s_clk, 1)

            def first(m, c, b, u):
                pool.wait_ge(s_ct, u)
                heads = clk[:, bass.ds(c * TPC, TPC), m * H // KT:(m + 1) * H // KT]
                g.tensor_copy(stage[:, b, :, :].rearrange("p t (h d) -> p t h d", d=DH),
                                      heads.rearrange("p t (h a) -> p t h a", a=1).to_broadcast([P, TPC, H // KT, DH])
                                      ).then_inc(s_stage, 1)

            def numerator(m, c, b, u):
                pool.wait_ge(s_div, u + 1)
                g.tensor_tensor(num[:, :], gt[:, m, bass.ds(c * CH, CH)], ge8[:, :], ALU.mult).then_inc(s_num, 1)

            def second(m, c, b, u):
                pool.wait_ge(s_rec, u + 1)
                g.tensor_tensor(rge[:, :], rec[:, b, :], pcs8[:, b, :], ALU.mult).then_inc(s_num, 1)
                pool.wait_ge(s_full, u)
                pool.wait_ge(s_num, 2 * u + 1)
                g.tensor_tensor(fac[:, 0, :], num[:, :], rec[:, b, :], ALU.mult)
                pool.wait_ge(s_num, 2 * u + 2)
                g.tensor_tensor(fac[:, 1, :], rge[:, :], pexp[:, b, :], ALU.mult).then_inc(s_fac, 1)

            def both(new, old):
                if new:
                    first(*new)
                if old:
                    second(*old)
                if new:
                    pool.wait_ge(s_fac, new[3])
                    numerator(*new)

            in_turn(pool, both)

        @block.tensor
        def _(pe):
            for m, c, b, u in units(pe):
                pe.wait_ge(s_stage, u + 1)
                pe.wait_ge(s_pe, u)
                for t in range(TPC):
                    ins = nc.tensor.transpose(ps_ct[:, b, t * P:(t + 1) * P], stage[:, b, t, :], keep["ident"][:, :])
                ins.then_inc(s_ct, 1)

        @block.vector
        def _(dve):
            v = nc.vector
            for m in range(KT):
                ins = v.tensor_reduce(npmax[:, m:m + 1], pt[:, m, :], AX.X, ALU.max, negate=True)
            ins.then_inc(s_max, 1)
            v.memset(onesr[:, :], 1.0)
            v.memset(pcarry[:, :], 0.0)
            st = Steps(dve, s_dve)
            dve.wait_ge(s_cabs, 3)
            st.step(v.tensor_scalar(clow[:, :, :], cexp[:, :, :], 1.0, -1.0, ALU.add, ALU.add))
            st.done()
            st.step(v.scalar_tensor_tensor(out=cln[:, :, :], in0=clow[:, :, :], scalar=0.0, in1=cln[:, :, :],
                                           op0=ALU.is_gt, op1=ALU.mult))
            st.done()
            st.step(v.tensor_tensor(clow[:, :, :], cexp[:, :, :], clow[:, :, :], ALU.subtract))
            st.done()
            st.step(v.tensor_tensor(cln[:, :, :], cln[:, :, :], clow[:, :, :], ALU.add))
            st.done()
            v.scalar_tensor_tensor(out=clk[:, :, :], in0=clk[:, :, :], scalar=0.0, in1=cln[:, :, :],
                                   op0=ALU.max, op1=ALU.add).then_inc(s_clk, 1)
            assert st.count == CLOCK_STEPS - 1

            def factors(m, c, b, u):
                def summands():
                    dve.wait_ge(s_pexp, u + 1)
                    dve.wait_ge(s_ct, u + 1)
                    if not (isinstance(u, int) and u == 0):
                        dve.wait_ge(s_fac, u - 1)
                    v.tensor_tensor(pexp[:, b, :], pe_x[:, b, :], ps_ct[:, b, :], ALU.mult).then_inc(s_pe, 1)

                def sums():
                    dve.wait_ge(s_pe, u + 1)
                    dve.wait_ge(s_carry, u)
                    v.tensor_tensor_scan(pcs[:, :], onesr[:, :], pexp[:, b, :], pcarry[:, m:m + 1], ALU.mult,
                                         ALU.add).then_inc(s_scan, 1)

                def divisors():
                    dve.wait_ge(s_scan, u + 1)
                    v.tensor_copy(pcarry[:, m:m + 1], pcs[:, CH - 1:CH]).then_inc(s_carry, 1)
                    v.tensor_scalar(pcs8[:, b, :], pcs[:, :], 1e-8, 1.0 / QSCALE, ALU.add, ALU.mult)
                    v.tensor_scalar(ge8[:, :], gt[:, m, bass.ds(c * CH, CH)], 1e-8, None, ALU.add).then_inc(s_div, 1)

                def inverse():
                    dve.wait_ge(s_div, u + 1)
                    v.tensor_tensor(ge_pcs[:, :], ge8[:, :], pcs8[:, b, :], ALU.mult).then_inc(s_prod, 1)
                    dve.wait_ge(s_prod, u + 1)
                    v.reciprocal(rec[:, b, :], ge_pcs[:, :]).then_inc(s_rec, 1)

                return summands, sums, divisors, inverse

            def split(m, c, b, u):
                def scale():
                    dve.wait_ge(s_in, 16 * (u + 1))
                    dve.wait_ge(s_fac, u + 1)
                    v.tensor_tensor(full[:, :, :], qk[:, b, :, :], fac[:, :, :], ALU.mult).then_inc(s_full, 1)

                def middle():
                    dve.wait_ge(s_hi, u + 1)
                    v.tensor_tensor(rest[:, :, :], full[:, :, :], parts[:, b, :, 0, :], ALU.subtract).then_inc(s_rest, 1)

                def low():
                    dve.wait_ge(s_mid, u + 1)
                    v.tensor_tensor(parts[:, b, :, 2, :], rest[:, :, :], parts[:, b, :, 1, :], ALU.subtract).then_inc(s_lo, 1)

                return scale, middle, low

            def both(new, old):
                summands, sums, divisors, inverse = factors(*new) if new else (None,) * 4
                scale, middle, low = split(*old) if old else (None,) * 3
                for piece in (summands, sums, scale, divisors, middle, inverse, low):
                    if piece:
                        piece()

            in_turn(dve, both)


def attention_phase(nc, a, keep):
    QUADS = [(c, g) for c in range(NCH) for g in range(c + 1)]
    NQ = len(QUADS)
    MUNITS = [(i, j) for i in range(NT) for j in range(i // TPC + 1)]
    assert len(MUNITS) == NQ * TPC
    NM = len(MUNITS)
    MRING = 3
    VW = 2 * DH
    with ExitStack() as ctx:
        def sb(name, shape, dt=F32):
            return ctx.enter_context(nc.sbuf_tensor(name, shape, dt))

        def psum(name, shape):
            return ctx.enter_context(nc.psum_tensor(name, shape, F32))

        def sem(name):
            return ctx.enter_context(nc.semaphore(name))

        qs = [sb(f"qs{b}", [P, T], BF16) for b in range(2)]
        ks = [sb(f"ks{b}", [P, T], BF16) for b in range(2)]
        vs = [sb(f"vs{b}", [P, NT, VW]) for b in range(2)]
        fold = sb("fold", [P, DH + 1])
        ident16 = sb("ident16", [P, P], BF16)
        mask_q = sb("mask_q", [P, P], BF16)
        mask_k = sb("mask_k", [P, CH + 3 * P], BF16)
        ex = [sb(f"ex{i}", [P, TPC, CH]) for i in range(3)]
        maxes = sb("maxes", [P, NM])
        nmax = sb("nmax", [P, NT])
        nrest = sb("nrest", [P, NT])
        nparts = sb("nparts", [P, PARTS, NT], BF16)
        nrows = sb("nrows", [PARTS * NT, P], BF16)
        osb = sb("osb", [P, 2, CH])
        rden = sb("rden", [P, TPC])

        ps_s = [psum(f"ps_s{i}", [P, 2, CH]) for i in range(2)]
        ps_m = [psum(f"ps_m{i}", [P, CH]) for i in range(MRING)]
        ps_o = psum("ps_o", [P, CH])

        s_const = sem("p3_const")
        s_ones = sem("p3_ones")
        s_load = sem("p3_load")
        s_vs = sem("p3_vs")
        s_mm = sem("p3_mm")
        s_mr = sem("p3_mr")
        s_st = sem("p3_st")
        s_ex = sem("p3_ex")
        s_pv = sem("p3_pv")
        s_osb = sem("p3_osb")
        s_dve = sem("p3_dve")
        s_np = sem("p3_np")
        s_nt = sem("p3_nt")
        s_nr = sem("p3_nr")
        s_nload = sem("p3_nload")
        NLOADS = 4
        parts = a["parts"].rearrange("w r (h d) n -> w r h d n", d=DH)
        att, v_all = keep["att"], keep["v"]

        MFROM, MTO = 5, NQ - 4

        def units_by(q):
            return min(NM, max(0, -(-NM * (q + 1 - MFROM) // (MTO - MFROM))))

        def plan(more):
            for q in range(NQ + 2):
                units = range(units_by(q - 1), units_by(q)) if more else []
                if q < NQ:
                    for half in range(2):
                        yield "scores", (q, half)
                        for u in units[2 * half:2 * half + 2]:
                            yield "unit", u
                if 1 <= q <= NQ:
                    yield "product", q - 1
                for u in units[4:]:
                    yield "unit", u
                if q == MTO + 1 and more:
                    yield "turn", 0
                if 2 <= q and QUADS[q - 2][0] == QUADS[q - 2][1]:
                    yield "fold", QUADS[q - 2][0]

        FIRST = NM + 1
        def uses(more):
            return [x for x in plan(more) if x[0] in ("unit", "turn", "fold")]

        NUSE = len(uses(True))
        assert NUSE == NM + NCH + 1 and NUSE % MRING == 0

        def use_of(h, more, what, n):
            return FIRST + h * NUSE + uses(more).index((what, n))

        MAX_STEPS = NCH + 3
        NLOAD = 2 * NPROD

        block = ctx.enter_context(nc.Block())

        def heads(engine):
            with engine.Fori(0, H // 2 - 1) as pair:
                for b in range(2):
                    yield pair * 2 + b, b, True
            yield H - 2, 0, True
            yield H - 1, 1, False

        @block.sync
        def _(sp):
            sp.dma_start(ident16[:, :], a["eye16"]).then_inc(s_const, 16)
            sp.dma_start(mask_q[:, :], a["mask_q"]).then_inc(s_const, 16)
            sp.dma_start(mask_k[:, :], a["mask_k"]).then_inc(s_const, 16)
            sp.dma_start(fold[:, :], a["fold"]).then_inc(s_const, 16)

            def load(h, b):
                for w, (which, to) in enumerate(((Q_PARTS, qs[b]), (K_PARTS, ks[b]))):
                    for row, part in enumerate(which):
                        sp.dma_start(to[row * DH:(row + 1) * DH, :],
                                     parts[w, part, bass.ds(h, 1)].rearrange("a d n -> (a d) n")).then_inc(s_load, 16)

            def rows_in(b, turned):
                sp.wait_ge(s_mr, turned)
                for r in range(PARTS):
                    sp.dma_start(qs[b][SROWS + r:SROWS + r + 1, :].rearrange("a (t n) -> a t n", n=P),
                                 nrows[r * NT:(r + 1) * NT, :]).then_inc(s_nload, 16)

            load(0, 0)
            rows_in(0, FIRST)
            for h, b, more in heads(sp):
                if more:
                    sp.wait_ge(s_pv, NQ * h)
                    load(h + 1, 1 - b)
                    rows_in(1 - b, use_of(h, True, "turn", 0) + 1)

        @block.gpsimd
        def _(pool):
            g = nc.gpsimd
            for b in range(2):
                g.memset(vs[b][:, :, DH:DH + 1], 1.0)
                g.memset(vs[b][:, :, DH + 1:], 0.0)

            def stage(h, b):
                g.tensor_copy(vs[b][:, :, 0:DH], v_all[:, :, bass.ds(h * DH, DH)]).then_inc(s_vs, 1)

            stage(0, 0)
            for h, b, more in heads(pool):
                if more:
                    pool.wait_ge(s_pv, NQ * h)
                    stage(h + 1, 1 - b)

        def osb_out(act, h, q, more):
            c = QUADS[q][0]
            act.wait_ge(s_pv, NQ * h + q + 1)
            act.wait_ge(s_mm, use_of(h, more, "fold", c - 2) + 1 if c >= 2 else FIRST + h * NUSE)
            nc.scalar.activation(osb[:, c % 2, :], ps_o[:, :], ACT.Copy).then_inc(s_osb, 1)

        @block.scalar
        def _(act):
            s = nc.scalar
            for h, b, more in heads(act):
                for q, (c, g) in enumerate(QUADS):
                    if q >= len(ex):
                        act.wait_ge(s_pv, NQ * h + q - len(ex) + 1)
                    else:
                        act.wait_ge(s_pv, NQ * h)
                    e = ex[q % len(ex)]
                    for half in range(2):
                        act.wait_ge(s_st, 2 * NQ * h + 2 * q + half + 1)
                        if g < c or c == 0:
                            ins = s.activation(e[:, 2 * half:2 * half + 2, :], ps_s[half][:, :, :], ACT.Exp,
                                               scale=DH ** -0.5 / QSCALE)
                        else:
                            for i in range(2):
                                j = 2 * half + i
                                ins = s.activation(e[:, j, j * P:], ps_s[half][:, i, j * P:], ACT.Exp, scale=DH ** -0.5 / QSCALE)
                        ins.then_inc(s_ex, 1)
                    if q >= 1 and QUADS[q - 1][0] != c:
                        osb_out(act, h, q - 1, more)
                osb_out(act, h, NQ - 1, more)

        @block.tensor
        def _(pe):
            t_ = nc.tensor
            pe.wait_ge(s_const, 16 * NLOADS)

            def slot_free(use):
                pe.wait_ge(s_mr, use - MRING + 1)

            def unit(b, u, slot):
                i, j = MUNITS[u]
                width = min(CH, (i + 1) * P - j * CH)
                diagonal = j == i // TPC
                ins = t_.matmul(ps_m[slot][:, 0:width], qs[b][0:SROWS, i * P:(i + 1) * P],
                                ks[b][0:SROWS, j * CH:j * CH + width], start=True, stop=not diagonal)
                if diagonal:
                    ins = t_.matmul(ps_m[slot][:, width - P:width], ident16[:, :], mask_q[:, :], start=False, stop=True)
                ins.then_inc(s_mm, 1)

            def turn(h, slot):
                pe.wait_ge(s_np, h + 1)
                t_.matmul(ps_m[slot][0:PARTS * NT, 0:P], nparts[:, :, :].rearrange("p r t -> p (r t)"), ident16[:, :],
                          start=True, stop=True).then_inc(s_mm, 1)

            def scores(b, q, half):
                c, g = QUADS[q]
                for i in range(2):
                    j = 2 * half + i
                    kb = TPC * g + j
                    off = j * P if g == c and c > 0 else 0
                    diagonal = g == c
                    ins = t_.matmul(ps_s[half][:, i, off:], ks[b][0:SROWS + PARTS, kb * P:(kb + 1) * P],
                                    qs[b][0:SROWS + PARTS, c * CH + off:(c + 1) * CH], start=True, stop=not diagonal)
                    if diagonal:
                        lo = 3 * P - j * P + off
                        wide = CH if c == 0 else P
                        ins = t_.matmul(ps_s[half][:, i, off:off + wide], ident16[:, :], mask_k[:, lo:lo + wide],
                                        start=False, stop=True)
                ins.then_inc(s_st, 1)

            def product(h, b, q):
                c, g = QUADS[q]
                if g == 0:
                    pe.wait_ge(s_osb, NCH * h + c)
                pe.wait_ge(s_ex, 2 * NQ * h + 2 * q + 2)
                for j in range(TPC):
                    off = j * P if g == c and c > 0 else 0
                    ins = t_.matmul(ps_o[j * VW:(j + 1) * VW, off:], vs[b][:, TPC * g + j, :],
                                    ex[q % len(ex)][:, j, off:], start=(g == 0), stop=(g == c))
                ins.then_inc(s_pv, 1)

            def folded(h, c, slot):
                pe.wait_ge(s_osb, NCH * h + c + 1)
                for t in range(TPC):
                    ins = t_.matmul(ps_m[slot][:, t * (DH + 1):(t + 1) * (DH + 1)], osb[:, c % 2, t * P:(t + 1) * P],
                                    fold[:, :], start=True, stop=True)
                ins.then_inc(s_mm, 1)

            pe.wait_ge(s_load, 16 * NLOAD)
            pe.wait_ge(s_ones, 1)
            for u in range(NM):
                if u >= MRING:
                    slot_free(u)
                unit(0, u, u % MRING)
            slot_free(NM)
            turn(0, NM % MRING)
            for h, b, more in heads(pe):
                pe.wait_ge(s_nload, 16 * PARTS * (h + 1))
                pe.wait_ge(s_vs, h + 1)
                k = 0
                for what, n in plan(more):
                    if what == "scores":
                        q, half = n
                        pe.wait_ge(s_ex, 2 * NQ * h + (2 * q + half - 1 if q else 0))
                        scores(b, q, half)
                        continue
                    if what == "product":
                        product(h, b, n)
                        continue
                    slot = (FIRST + (0 if more else NUSE) + k) % MRING
                    if what == "unit" and n == 0:
                        pe.wait_ge(s_load, 16 * NLOAD * (h + 2))
                    slot_free(FIRST + h * NUSE + k)
                    if what == "unit":
                        unit(1 - b, n, slot)
                    elif what == "turn":
                        turn(h + 1, slot)
                    else:
                        folded(h, n, slot)
                    k += 1

        @block.vector
        def _(dve):
            v = nc.vector

            def unit_max(st, use, u, slot):
                i, j = MUNITS[u]
                width = min(CH, (i + 1) * P - j * CH)
                dve.wait_ge(s_mm, use + 1)
                v.tensor_reduce(maxes[:, u:u + 1], ps_m[slot][:, 0:width], AX.X, ALU.max).then_inc(s_mr, 1)
                c = i // TPC
                if i % TPC == TPC - 1 and j == c:
                    dve.wait_ge(s_mr, use + 1)
                    st.step(v.tensor_reduce(nmax[:, TPC * c:TPC * (c + 1)],
                                            maxes[:, u + 1 - TPC * (c + 1):u + 1].rearrange("p (t j) -> p t j", j=c + 1),
                                            AX.X, ALU.max, negate=True))
                if u == NM - 1:
                    split_maxima(st)

            def split_maxima(st):
                st.done()
                st.step(v.tensor_copy(nparts[:, 0, :], nmax[:, :]))
                st.done()
                st.step(v.tensor_tensor(nrest[:, :], nmax[:, :], nparts[:, 0, :], ALU.subtract))
                st.done()
                st.step(v.tensor_copy(nparts[:, 1, :], nrest[:, :]))
                st.done()
                v.tensor_tensor(nparts[:, 2, :], nrest[:, :], nparts[:, 1, :], ALU.subtract).then_inc(s_np, 1)

            def turned_rows(h, use, slot):
                dve.wait_ge(s_mm, use + 1)
                dve.wait_ge(s_nload, 16 * PARTS * h)
                v.tensor_copy(nrows[:, :], ps_m[slot][0:PARTS * NT, 0:P]).then_inc(s_mr, 1)

            def normalise(st, h, use, c, slot):
                dve.wait_ge(s_mm, use + 1)
                o = ps_m[slot][:, 0:TPC * (DH + 1)].rearrange("p (t d) -> p t d", d=DH + 1)
                dve.wait_ge(s_mr, use)
                st.step(v.reciprocal(rden[:, :], o[:, :, DH]))
                st.done()
                v.tensor_tensor(att[:, TPC * c:TPC * (c + 1), bass.ds(h * DH, DH)], o[:, :, 0:DH],
                                rden[:, :].rearrange("p (t a) -> p t a", a=1).to_broadcast([P, TPC, DH]),
                                ALU.mult).then_inc(s_mr, 1)

            for b in range(2):
                ins = v.memset(ks[b][SROWS:SROWS + PARTS, :], 1.0)
            ins.then_inc(s_ones, 1)
            st = Steps(dve, s_dve)
            for u in range(NM):
                unit_max(st, u, u, u % MRING)
            assert st.count == MAX_STEPS
            turned_rows(0, NM, NM % MRING)
            for h, b, more in heads(dve):
                st = Steps(dve, s_dve, MAX_STEPS + h * (MAX_STEPS + NCH))
                for k, (what, n) in enumerate(uses(more)):
                    use = FIRST + h * NUSE + k
                    slot = (FIRST + (0 if more else NUSE) + k) % MRING
                    if what == "unit":
                        unit_max(st, use, n, slot)
                    elif what == "turn":
                        turned_rows(h + 1, use, slot)
                    else:
                        normalise(st, h, use, n, slot)
                assert st.count == (MAX_STEPS if more else 0) + NCH


class Norm:

    def __init__(self, nc, sb, sem, name):
        self.v = nc.vector
        self.stats = sb(f"{name}_stats", [P, TPC, 6])
        self.mv = sb(f"{name}_mv", [P, TPC, 2])
        self.rstd = sb(f"{name}_rstd", [P, TPC])
        self.spare = sb(f"{name}_spare", [P, 1])
        self.veps = sb(f"{name}_veps", [P, TPC])
        self.eps = sb(f"{name}_eps", [P, TPC])
        self.power = sb(f"{name}_power", [P, TPC])
        self.s_var, self.s_veps, self.s_rstd = sem(f"{name}_var"), sem(f"{name}_veps"), sem(f"{name}_rstd")

    def constants(self):
        self.v.memset(self.eps[:, :], EPS)
        return self.v.memset(self.power[:, :], -0.5)

    def rows(self, dve, st, nth, src, out, out_sem=None):
        for t in range(TPC):
            ins = self.v.bn_stats(self.stats[:, t, :], src[:, t, :])
        st.step(ins)
        st.done()
        st.step(self.v.memset(self.spare[:, :], 0.0))
        for t in range(TPC):
            ins = self.v.bn_aggr(self.mv[:, t, :], self.stats[:, t, :])
        ins.then_inc(self.s_var, 1)
        dve.wait_ge(self.s_rstd, nth + 1)
        for t in range(TPC):
            ins = self.v.tensor_scalar(out[:, t, :], src[:, t, :], self.mv[:, t, 0:1], self.rstd[:, t:t + 1],
                                       ALU.subtract, ALU.mult)
        if out_sem is None:
            st.step(ins)
            st.done()
        else:
            ins.then_inc(out_sem, 1)

    def root(self, nc, pool, nth):
        pool.wait_ge(self.s_var, nth + 1)
        nc.gpsimd.tensor_tensor(self.veps[:, :], self.mv[:, :, 1], self.eps[:, :], ALU.add).then_inc(self.s_veps, 1)
        pool.wait_ge(self.s_veps, nth + 1)
        nc.gpsimd.tensor_tensor(self.rstd[:, :], self.veps[:, :], self.power[:, :], ALU.pow).then_inc(self.s_rstd, 1)


def mlp_phase(nc, a, keep):
    NORMS = 3
    NORM_STEPS = 2
    STEPS = 20
    with ExitStack() as ctx:
        def sb(name, shape, dt=F32):
            return ctx.enter_context(nc.sbuf_tensor(name, shape, dt))

        def psum(name, shape):
            return ctx.enter_context(nc.psum_tensor(name, shape, F32))

        def sem(name):
            return ctx.enter_context(nc.semaphore(name))

        out_w = sb("out_w", [P, KT, D])
        w1 = sb("w1", [P, KT, FF])
        w2 = sb("w2", [P, FT, D])
        rw = sb("rw", [P, KT, NE])
        g2 = sb("g2", [P, KT])
        b2 = sb("b2", [P, KT])
        bias1 = sb("bias1", [P, FT])
        out_b = sb("out_b", [P, D])
        bias2 = sb("bias2", [P, D])
        score_b = sb("score_b", [P, NE])
        experts = sb("experts", [P, NE])
        atts = sb("atts", [P, TPC, D])
        x0c = sb("x0c", [P, TPC, D])
        xc = sb("xc", [P, TPC, D])
        x1 = sb("x1", [P, TPC, D])
        wide = sb("wide", [P, TPC, D])
        wide_in = sb("wide_in", [P, TPC, D])
        turned = sb("turned", [P, KT, CH])
        turned_in = sb("turned_in", [P, KT, CH])
        hid = sb("hid", [P, FT, CH])
        lg = sb("lg", [P, TPC, NE])
        rwt = sb("rwt", [P, TPC, NE])
        cor = sb("cor", [P, TPC, NE])
        small = sb("small", [P, TPC])
        top = sb("top", [P, TPC, 8])
        topi = sb("topi", [P, TPC, 8], U32)
        topf = sb("topf", [P, TPC, 8])
        hit = sb("hit", [P, TPC, NE, TOPK])
        ones = sb("ones", [P, 1])
        norm = Norm(nc, sb, sem, "p4")

        ps_t = psum("ps_t", [P, KT, CH])
        ps_y = psum("ps_y", [P, TPC, D])
        ps_h = psum("ps_h", [P, 2, CH])
        ps_r = psum("ps_r", [P, CH])
        ps_c = psum("ps_c", [P, CH])

        s_const = sem("p4_const")
        s_const2 = sem("p4_const2")
        s_in = sem("p4_in")
        s_xin = sem("p4_xin")
        s_dve = sem("p4_dve")
        s_t1, s_t2, s_t3 = sem("p4_t1"), sem("p4_t2"), sem("p4_t3")
        s_c1, s_c2, s_c3 = sem("p4_c1"), sem("p4_c2"), sem("p4_c3")
        s_y1, s_y2 = sem("p4_y1"), sem("p4_y2")
        s_x0b = sem("p4_x0b")
        s_x1 = sem("p4_x1")
        s_ln2 = sem("p4_ln2")
        s_x1b = sem("p4_x1b")
        s_h = sem("p4_h")
        s_gelu = sem("p4_gelu")
        s_mlp = sem("p4_mlp")
        s_nm = sem("p4_nm")
        s_x2 = sem("p4_x2")
        s_x2out = sem("p4_x2out")
        s_x3 = sem("p4_x3")
        s_hi = sem("p4_hi")
        s_lo = sem("p4_lo")
        s_lg = sem("p4_lg")
        s_lmax = sem("p4_lmax")
        s_lexp = sem("p4_lexp")
        s_hit = sem("p4_hit")
        s_cnt = sem("p4_cnt")
        s_cntout = sem("p4_cntout")
        NLOADS = 11

        x_dram = a["x"].rearrange("a (c t p) d -> c (a p) t d", t=TPC, p=P)
        x0_dram = a["x0"].rearrange("(c t p) d -> c p t d", t=TPC, p=P)
        x2_dram = a["x2"].rearrange("(c t p) d -> c p t d", t=TPC, p=P)
        x3h, x3l, comb = keep["x3h"], keep["x3l"], keep["comb"]
        ident = keep["ident"]
        block = ctx.enter_context(nc.Block())

        def row_of(x):
            return x[:, :].rearrange("p (a d) -> p a d", a=1).to_broadcast([P, TPC, D])

        @block.sync
        def _(sp):
            for to, src in ((out_w, by_part(a["out_w"])), (w1, by_part(a["w1"])), (w2, by_part(a["w2"])),
                            (rw, by_part(a["router_w"])), (g2, a["ln2_g"]), (b2, a["ln2_b"]), (bias1, a["b1"]),
                            (out_b, a["out_b"]), (bias2, a["b2"]), (score_b, a["score_bias"]),
                            (experts, a["experts"])):
                sp.dma_start(to[:], src).then_inc(s_const, 16)

            def load(c):
                sp.dma_start(atts[:, :, :], keep["att"][:, bass.ds(c * TPC, TPC), :]).then_inc(s_in, 16)
                sp.dma_start(x0c[:, :, :], x0_dram[bass.ds(c, 1)].rearrange("a p t d -> p (a t) d")).then_inc(s_in, 16)

            load(0)
            with sp.Fori(1, NCH) as c:
                sp.wait_ge(s_x1, c)
                load(c)

        @block.gpsimd
        def _(pool):
            g = nc.gpsimd
            pool.dma_start(xc[:, :, :], x_dram[0]).then_inc(s_xin, 16)
            pool.wait_ge(s_const, 16 * NLOADS)
            pool.wait_ge(s_const2, 1)

            def first_bias(c):
                pool.wait_ge(s_in, 32 * (c + 1))
                g.tensor_tensor(x0c[:, :, :], x0c[:, :, :], row_of(out_b), ALU.add).then_inc(s_x0b, 1)

            def second_bias(c):
                pool.wait_ge(s_ln2, c + 1)
                g.tensor_tensor(x1[:, :, :], x1[:, :, :], row_of(bias2), ALU.add).then_inc(s_x1b, 1)

            def residual(c):
                pool.wait_ge(s_nm, c + 1)
                pool.wait_ge(s_xin, 16 * (c + 1))
                g.tensor_tensor(xc[:, :, :], xc[:, :, :], wide[:, :, :], ALU.add).then_inc(s_x2, 1)
                pool.wait_ge(s_x2, c + 1)
                pool.dma_start(x2_dram[bass.ds(c, 1)].rearrange("a p t d -> p (a t) d"), xc[:, :, :]).then_inc(s_x2out, 16)

            def low(c):
                pool.wait_ge(s_hi, c + 1)
                g.tensor_tensor(x3l[:, :, bass.ds(c * CH, CH)], turned[:, :, :],
                                x3h[:, :, bass.ds(c * CH, CH)].bitcast(F32), ALU.subtract).then_inc(s_lo, 1)

            first_bias(0)
            norm.root(nc, pool, 0)
            second_bias(0)
            with pool.Fori(0, NCH - 1) as c:
                first_bias(c + 1)
                norm.root(nc, pool, NORMS * c + 1)
                residual(c)
                norm.root(nc, pool, NORMS * c + 2)
                norm.root(nc, pool, NORMS * c + 3)
                second_bias(c + 1)
                low(c)
                pool.wait_ge(s_x2out, 16 * (c + 1))
                pool.wait_ge(s_x3, c + 1)
                pool.dma_start(xc[:, :, :], x_dram[bass.ds(c + 1, 1)].rearrange("a p t d -> p (a t) d")).then_inc(s_xin, 16)
            norm.root(nc, pool, NORMS * (NCH - 1) + 1)
            residual(NCH - 1)
            norm.root(nc, pool, NORMS * (NCH - 1) + 2)
            low(NCH - 1)
            pool.wait_ge(s_x2out, 16 * NCH)

        @block.scalar
        def _(act):
            s = nc.scalar
            act.wait_ge(s_const, 16 * NLOADS)

            def copy_attention(c):
                act.wait_ge(s_t1, c + 1)
                s.activation(turned_in[:, :, :], ps_t[:, :, :], ACT.Copy).then_inc(s_c1, 1)

            def copy_norm(c):
                act.wait_ge(s_y1, c + 1)
                act.wait_ge(s_t2, c + 1)
                for m in range(KT):
                    ins = s.activation(turned_in[:, m, :], ps_t[:, m, :], ACT.Identity, bias=b2[:, m:m + 1],
                                       scale=g2[:, m:m + 1])
                ins.then_inc(s_c2, 1)

            def hidden(c):
                act.wait_ge(s_y2, c)
                for f in range(FT):
                    act.wait_ge(s_h, FT * c + f + 1)
                    s.activation(hid[:, f, :], ps_h[:, f % 2, :], ACT.Gelu, bias=bias1[:, f:f + 1]).then_inc(s_gelu, 1)

            def copy_x3(c):
                act.wait_ge(s_lo, c)
                act.wait_ge(s_lg, c)
                act.wait_ge(s_t3, c + 1)
                s.activation(turned[:, :, :], ps_t[:, :, :], ACT.Copy).then_inc(s_c3, 1)
                s.activation(x3h[:, :, bass.ds(c * CH, CH)], ps_t[:, :, :], ACT.Copy).then_inc(s_hi, 1)

            def exponentials(c):
                act.wait_ge(s_lmax, c + 1)
                s.activation(rwt[:, :, :], lg[:, :, :], ACT.Exp).then_inc(s_lexp, 1)

            copy_attention(0)
            copy_norm(0)
            with act.Fori(0, NCH - 1) as c:
                hidden(c)
                copy_attention(c + 1)
                copy_x3(c)
                copy_norm(c + 1)
                exponentials(c)
            hidden(NCH - 1)
            copy_x3(NCH - 1)
            exponentials(NCH - 1)

        @block.tensor
        def _(pe):
            t_ = nc.tensor
            pe.wait_ge(s_const, 16 * NLOADS)

            def turn(src, sem):
                for t in range(TPC):
                    for m in range(KT):
                        ins = t_.transpose(ps_t[:, m, t * P:(t + 1) * P], src[:, t, m * P:(m + 1) * P], ident[:, :])
                ins.then_inc(sem, 1)

            def project(c):
                pe.wait_ge(s_in, 32 * (c + 1))
                turn(atts, s_t1)
                pe.wait_ge(s_mlp, c)
                pe.wait_ge(s_c1, c + 1)
                for t in range(TPC):
                    for k in range(KT):
                        ins = t_.matmul(ps_y[:, t, :], turned_in[:, k, t * P:(t + 1) * P], out_w[:, k, :],
                                        start=(k == 0), stop=(k == KT - 1))
                ins.then_inc(s_y1, 1)

            def turn_norm(c):
                pe.wait_ge(s_hi, c)
                pe.wait_ge(s_ln2, c + 1)
                turn(wide_in, s_t2)

            def mlp(c, between=None):
                pe.wait_ge(s_c2, c + 1)
                for f in range(FT):
                    pe.wait_ge(s_gelu, FT * c + (f - 1 if f >= 2 else 0))
                    for k in range(KT):
                        ins = t_.matmul(ps_h[:, f % 2, :], w1[:, k, f * P:(f + 1) * P], turned_in[:, k, :],
                                        start=(k == 0), stop=(k == KT - 1))
                    ins.then_inc(s_h, 1)
                if between:
                    between()
                pe.wait_ge(s_x1, c + 1)
                pe.wait_ge(s_gelu, FT * (c + 1))
                for t in range(TPC):
                    for f in range(FT):
                        ins = t_.matmul(ps_y[:, t, :], hid[:, f, t * P:(t + 1) * P], w2[:, f, :],
                                        start=(f == 0), stop=(f == FT - 1))
                ins.then_inc(s_y2, 1)

            def router(c):
                pe.wait_ge(s_x3, c + 1)
                turn(wide, s_t3)
                pe.wait_ge(s_c3, c + 1)
                pe.wait_ge(s_lmax, c)
                for t in range(TPC):
                    for k in range(KT):
                        ins = t_.matmul(ps_r[:, t * NE:(t + 1) * NE], turned[:, k, t * P:(t + 1) * P], rw[:, k, :],
                                        start=(k == 0), stop=(k == KT - 1))
                ins.then_inc(s_lg, 1)

            def count(c):
                pe.wait_ge(s_hit, c + 1)
                pe.wait_ge(s_cntout, c)
                for t in range(TPC):
                    ins = t_.matmul(ps_c[0:1, 0:NE], ones[:, :], cor[:, t, :], start=(t == 0), stop=(t == TPC - 1))
                ins.then_inc(s_cnt, 1)

            project(0)
            turn_norm(0)
            mlp(0)
            with pe.Fori(0, NCH - 1) as c:
                project(c + 1)
                router(c)
                turn_norm(c + 1)
                mlp(c + 1, between=lambda: count(c))
            router(NCH - 1)
            count(NCH - 1)

        @block.vector
        def _(dve):
            v = nc.vector
            v.memset(ones[:, :], 1.0)
            v.memset(comb[:, NE:FILLER, :], 1.0)
            v.memset(comb[:, FILLER, :], 0.0)
            norm.constants().then_inc(s_const2, 1)
            dve.wait_ge(s_const2, 1)
            dve.wait_ge(s_const, 16 * NLOADS)

            def over(x, n):
                return x.rearrange("p (t a) -> p t a", a=1).to_broadcast([P, TPC, n])

            def before_mlp(st, c, nth):
                dve.wait_ge(s_nm, c)
                dve.wait_ge(s_x0b, c + 1)
                dve.wait_ge(s_y1, c + 1)
                v.tensor_tensor(x1[:, :, :], ps_y[:, :, :], x0c[:, :, :], ALU.add).then_inc(s_x1, 1)
                dve.wait_ge(s_x1, c + 1)
                norm.rows(dve, st, nth, x1, wide_in, s_ln2)

            def after_mlp(st, c, nth):
                dve.wait_ge(s_x1b, c + 1)
                dve.wait_ge(s_y2, c + 1)
                v.tensor_tensor(x1[:, :, :], ps_y[:, :, :], x1[:, :, :], ALU.add).then_inc(s_mlp, 1)
                dve.wait_ge(s_mlp, c + 1)
                norm.rows(dve, st, nth, x1, wide, s_nm)

            def route(st, c, nth):
                def step(ins):
                    st.step(ins)
                    st.done()

                dve.wait_ge(s_x2, c + 1)
                norm.rows(dve, st, nth, xc, wide, s_x3)
                dve.wait_ge(s_lg, c + 1)
                logits = ps_r[:, 0:TPC * NE].rearrange("p (t e) -> p t e", e=NE)
                step(v.tensor_reduce(small[:, :], logits, AX.X, ALU.max))
                v.tensor_tensor(lg[:, :, :], logits, over(small[:, :], NE), ALU.subtract).then_inc(s_lmax, 1)
                dve.wait_ge(s_lexp, c + 1)
                step(v.tensor_reduce(small[:, :], rwt[:, :, :], AX.X, ALU.add))
                step(v.reciprocal(small[:, :], small[:, :]))
                step(v.tensor_tensor(rwt[:, :, :], rwt[:, :, :], over(small[:, :], NE), ALU.mult))
                step(v.tensor_tensor(cor[:, :, :], rwt[:, :, :],
                                     score_b[:, :].rearrange("p (a e) -> p a e", a=1).to_broadcast([P, TPC, NE]), ALU.add))
                v.memset(norm.spare[:, :], 0.0)
                for t in range(TPC):
                    ins = v.max(top[:, t, :], cor[:, t, :])
                step(ins)
                st.step(v.memset(norm.spare[:, :], 1.0))
                for t in range(TPC):
                    ins = v.max_index(topi[:, t, :], top[:, t, :], cor[:, t, :])
                step(ins)
                step(v.tensor_copy(topf[:, :, :], topi[:, :, :]))
                step(v.tensor_tensor(hit[:, :, :, :],
                                     experts[:, :].rearrange("p (a e k) -> p a e k", a=1, k=1).to_broadcast([P, TPC, NE, TOPK]),
                                     topf[:, :, 0:TOPK].rearrange("p t (a k) -> p t a k", a=1).to_broadcast([P, TPC, NE, TOPK]),
                                     ALU.is_equal))
                v.tensor_reduce(cor[:, :, :], hit[:, :, :, :], AX.X, ALU.add).then_inc(s_hit, 1)
                dve.wait_ge(s_hit, c + 1)
                step(v.tensor_tensor(rwt[:, :, :], rwt[:, :, :], cor[:, :, :], ALU.mult))
                step(v.tensor_reduce(small[:, :], rwt[:, :, :], AX.X, ALU.add))
                dve.wait_ge(s_cnt, c + 1)
                v.tensor_copy(keep["counts"][0:1, bass.ds(c * NE, NE)], ps_c[0:1, 0:NE]).then_inc(s_cntout, 1)
                step(v.tensor_scalar(small[:, :], small[:, :], 1e-12, None, ALU.max))
                step(v.reciprocal(small[:, :], small[:, :]))
                v.tensor_tensor(comb[:, 0:NE, bass.ds(c * TPC, TPC)].rearrange("p e t -> p t e"), rwt[:, :, :],
                                over(small[:, :], NE), ALU.mult)

            before_mlp(Steps(dve, s_dve), 0, 0)
            with dve.Fori(0, NCH - 1) as c:
                st = Steps(dve, s_dve, c * STEPS + NORM_STEPS)
                after_mlp(st, c, NORMS * c + 1)
                before_mlp(st, c + 1, NORMS * c + 2)
                route(st, c, NORMS * c + 3)
                assert st.count == STEPS, st.count
            st = Steps(dve, s_dve, (NCH - 1) * STEPS + NORM_STEPS)
            after_mlp(st, NCH - 1, NORMS * (NCH - 1) + 1)
            route(st, NCH - 1, NORMS * (NCH - 1) + 2)


def list_phase(nc, a, keep):
    with ExitStack() as ctx:
        def sb(name, shape, dt=F32):
            return ctx.enter_context(nc.sbuf_tensor(name, shape, dt))

        def sem(name):
            return ctx.enter_context(nc.semaphore(name))

        HALVES = NCH * NE // P
        one = sb("one", [P, P])
        upto = sb("upto", [P, P])
        places = sb("places", [P, NCH * NE])
        codes = sb("codes", [P, HALVES, 2])
        counts_row = sb("counts_row", [1, NCH * NE])
        chosen = sb("chosen", [P, HALVES])
        rank = sb("rank", [P, HALVES + 1])
        starts = sb("starts", [1, NCH * NE // ROUND])
        count = sb("count", [1, 1])
        at_place = sb("at_place", [P, HALVES, NCH * NE])
        psum = ctx.enter_context(nc.psum_tensor("ps_list", [P, 3, CH], F32))
        s_const = sem("l_const")
        s_one = sem("l_one")
        s_row = sem("l_row")
        s_col = sem("l_col")
        s_chosen = sem("l_chosen")
        s_rank = sem("l_rank")
        s_place = sem("l_place")
        s_list = sem("l_list")
        s_rk = sem("l_rk")
        block = ctx.enter_context(nc.Block())
        listed, more_rounds = keep["listed"], keep["more_rounds"]

        @block.sync
        def _(sp):
            for to, src in ((upto[:, :], a["upto"]), (places[:, :], a["places"]), (codes[:, :, :], a["codes"]),
                            (listed[:, :, :], a["listed"])):
                sp.dma_start(to, src).then_inc(s_const, 16)

        @block.tensor
        def _(pe):
            t_ = nc.tensor
            pe.wait_ge(s_one, 1)
            pe.wait_ge(s_row, 1)
            for h in range(HALVES):
                ins = t_.matmul(psum[:, 0, h:h + 1], counts_row[0:1, h * P:(h + 1) * P], one[0:1, 0:1], start=True, stop=True)
            ins.then_inc(s_col, 1)
            pe.wait_ge(s_chosen, 1)
            pe.wait_ge(s_const, 64)
            for h in range(HALVES):
                for k in range(h + 1):
                    ins = t_.matmul(psum[:, 1, h:h + 1], (upto if k == h else one)[:, :], chosen[:, k:k + 1],
                                    start=(k == 0), stop=(k == h))
            for k in range(HALVES):
                ins = t_.matmul(psum[:, 1, HALVES:HALVES + 1], one[:, :], chosen[:, k:k + 1], start=(k == 0),
                                stop=(k == HALVES - 1))
            ins.then_inc(s_rank, 1)
            pe.wait_ge(s_place, 1)
            for n in range(2):
                for k in range(HALVES):
                    ins = t_.matmul(psum[0:1, 2, n * NCH * NE:(n + 1) * NCH * NE], codes[:, k, n:n + 1], at_place[:, k, :],
                                    start=(k == 0), stop=(k == HALVES - 1))
            ins.then_inc(s_list, 1)

        @block.vector
        def _(dve):
            v = nc.vector
            v.memset(one[:, :], 1.0).then_inc(s_one, 1)
            v.tensor_copy(counts_row[0:1, :], keep["counts"][0:1, :]).then_inc(s_row, 1)
            dve.wait_ge(s_col, 1)
            v.tensor_scalar(chosen[:, :], psum[:, 0, 0:HALVES], 0.0, None, ALU.is_gt).then_inc(s_chosen, 1)
            dve.wait_ge(s_rank, 1)
            v.tensor_copy(rank[:, :], psum[:, 1, 0:HALVES + 1]).then_inc(s_rk, 1)
            dve.wait_ge(s_rk, 1)
            dve.wait_ge(s_chosen, 1)
            dve.wait_ge(s_const, 64)
            for h in range(HALVES):
                ins = v.tensor_scalar(at_place[:, h, :], places[:, :], rank[:, h:h + 1], chosen[:, h:h + 1],
                                      ALU.is_equal, ALU.mult)
            ins.then_inc(s_place, 1)
            v.tensor_scalar(starts[0:1, :], places[0:1, :].rearrange("a (r i) -> a r i", i=ROUND)[:, :, 0],
                            rank[0:1, HALVES:HALVES + 1], None, ALU.is_le).then_inc(s_rk, 1)
            dve.wait_ge(s_rk, 2)
            v.tensor_reduce(count[0:1, :], starts[0:1, :], AX.X, ALU.add).then_inc(s_rk, 1)
            dve.wait_ge(s_rk, 3)
            v.tensor_scalar(more_rounds[0:1, :], count[0:1, :], float(FIXED // ROUND - 1), None, ALU.add)
            dve.wait_ge(s_list, 1)
            v.tensor_scalar(listed[0:1, 0, FIXED:FIXED + NCH * NE], psum[0:1, 2, 0:NCH * NE], float(FILLER), None, ALU.add)
            v.tensor_copy(listed[0:1, 1, FIXED:FIXED + NCH * NE], psum[0:1, 2, NCH * NE:])


def expert_phase(nc, a, keep):
    GU = KT * 2 * NI
    EW = GU + D
    ROUNDS = (FIXED + NCH * NE) // ROUND
    with ExitStack() as ctx:
        def sb(name, shape, dt=F32):
            return ctx.enter_context(nc.sbuf_tensor(name, shape, dt))

        def psum(name, shape):
            return ctx.enter_context(nc.psum_tensor(name, shape, F32))

        def sem(name):
            return ctx.enter_context(nc.semaphore(name))

        raw = [sb(f"raw{i}", [P, EW]) for i in range(ROUND)]
        wh = [sb(f"wh{i}", [P, EW], F32R) for i in range(ROUND)]
        wl = [sb(f"wl{i}", [P, EW], F32R) for i in range(ROUND)]
        sg = [sb(f"sg{i}", [P, CH]) for i in range(2)]
        hh = [sb(f"hh{i}", [P, CH]) for i in range(2)]
        hhi = [sb(f"hhi{i}", [P, CH], F32R) for i in range(2)]
        hlo = [sb(f"hlo{i}", [P, CH], F32R) for i in range(2)]
        y, x3h, x3l, comb = keep["y"], keep["x3h"], keep["x3l"], keep["comb"]
        listed = keep["listed"]

        ps_g = [psum(f"ps_g{i}", [P, CH]) for i in range(2)]
        ps_u = [psum(f"ps_u{i}", [P, CH]) for i in range(2)]
        ps_y = [psum(f"ps_yy{i}", [P, TPC, D]) for i in range(2)]

        s_zero = sem("p5_zero")
        s_raw = [sem(f"p5_raw{i}") for i in range(ROUND)]
        s_wh = sem("p5_wh")
        s_wl = sem("p5_wl")
        s_gu = sem("p5_gu")
        s_silu = sem("p5_silu")
        s_hh = sem("p5_hh")
        s_hhi = sem("p5_hhi")
        s_hlo = sem("p5_hlo")
        s_dn = sem("p5_dn")
        s_yy = sem("p5_yy")
        AHEAD = 2
        block = ctx.enter_context(nc.Block())

        def loaded(engine, which, u, limit):
            return engine.value_load(listed[0:1, which, bass.ds(u, 1)], min_val=0, max_val=limit)

        def rounds(engine, step, finish):
            for i in range(ROUND):
                step(i, i)
            after_first = engine.value_load(keep["more_rounds"][0:1, 0:1], min_val=0, max_val=ROUNDS - 1)
            with engine.Fori(1, ROUNDS) as r:
                with engine.If(r <= after_first):
                    for i in range(ROUND):
                        step(r * ROUND + i, i)
            finish(after_first * ROUND + ROUND)

        def wait_past(engine, sem, u, back):
            if not isinstance(u, int):
                engine.wait_ge(sem, u + (1 - back))
            elif u >= back:
                engine.wait_ge(sem, u + 1 - back)

        @block.sync
        def _(sp):
            def load(u, i):
                wait_past(sp, s_wl, u, ROUND)
                e = loaded(sp, 0, u, FILLER)
                sp.dma_start(raw[i][:, :], a["experts_w"][bass.ds(e, 1)].rearrange("a p n -> p (a n)")).then_inc(s_raw[i], 16)

            def finish(n):
                for i in range(AHEAD):
                    sp.wait_ge(s_wl, n + i - ROUND + 1)
                    sp.dma_start(raw[i][:, :], a["experts_w"][FILLER]).then_inc(s_raw[i], 16)

            rounds(sp, load, finish)

        @block.scalar
        def _(act):
            s = nc.scalar

            def high(u, i):
                act.wait_ge(s_raw[i], (16 // ROUND) * (u - i) + 16)
                wait_past(act, s_dn, u, ROUND)
                s.activation(wh[i][:, :], raw[i][:, :], ACT.Copy).then_inc(s_wh, 1)

            def step(u, i):
                b = i % 2
                act.wait_ge(s_gu, u + 1)
                wait_past(act, s_hh, u, 2)
                s.activation(sg[b][:, :], ps_g[b][:, :], ACT.Silu).then_inc(s_silu, 1)
                act.wait_ge(s_hh, u + 1)
                wait_past(act, s_dn, u, 2)
                s.activation(hhi[b][:, :], hh[b][:, :], ACT.Copy).then_inc(s_hhi, 1)
                high(u + AHEAD, (i + AHEAD) % ROUND)

            for i in range(AHEAD):
                high(i, i)
            rounds(act, step, lambda n: None)

        @block.gpsimd
        def _(pool):
            g = nc.gpsimd

            def low(u, i):
                pool.wait_ge(s_wh, u + 1)
                g.tensor_tensor(wl[i][:, :], raw[i][:, :], wh[i][:, :].bitcast(F32), ALU.subtract).then_inc(s_wl, 1)

            def step(u, i):
                b = i % 2
                pool.wait_ge(s_hhi, u + 1)
                g.tensor_tensor(hlo[b][:, :], hh[b][:, :], hhi[b][:, :].bitcast(F32), ALU.subtract).then_inc(s_hlo, 1)
                low(u + AHEAD, (i + AHEAD) % ROUND)

            for i in range(AHEAD):
                low(i, i)
            rounds(pool, step, lambda n: None)

        @block.tensor
        def _(pe):
            t_ = nc.tensor

            def three(out, l, r, start, stop):
                for n, (x, w) in enumerate(((0, 0), (0, 1), (1, 0))):
                    ins = t_.matmul(out, l[x], r[w], start=start and n == 0, stop=stop and n == 2, skip_group_check=True)
                return ins

            def down(u, i):
                b = i % 2
                pe.wait_ge(s_hlo, u + 1)
                wait_past(pe, s_yy, u, 2)
                w = slice(GU, GU + D)
                for t in range(TPC):
                    tk = slice(t * P, (t + 1) * P)
                    ins = three(ps_y[b][:, t, :], (hhi[b][:, tk], hlo[b][:, tk]), (wh[i][:, w], wl[i][:, w]),
                                t % 2 == 0, True)
                ins.then_inc(s_dn, 1)

            def step(u, i):
                b = i % 2
                c = loaded(pe, 1, u, NCH - 1)
                tok = bass.ds(c * CH, CH)
                pe.wait_ge(s_wl, u + 1)
                wait_past(pe, s_hh, u, 2)
                for n, to in enumerate((ps_g[b], ps_u[b])):
                    for k in range(KT):
                        lo = (k * 2 + n) * NI
                        ins = three(to[:, :], (wh[i][:, lo:lo + NI], wl[i][:, lo:lo + NI]), (x3h[:, k, tok], x3l[:, k, tok]),
                                    k == 0, k == KT - 1)
                ins.then_inc(s_gu, 1)
                if not (isinstance(u, int) and u == 0):
                    down(u - 1, (i - 1) % ROUND)

            rounds(pe, step, lambda n: down(n - 1, ROUND - 1))

        @block.vector
        def _(dve):
            v = nc.vector
            weights = comb[:, :, :].rearrange("p e n -> p (e n)")
            v.memset(y[:, :, :], 0.0).then_inc(s_zero, 1)

            def add_up(u, i):
                b = i % 2
                e = loaded(dve, 0, u, FILLER)
                c = loaded(dve, 1, u, NCH - 1)
                dve.wait_ge(s_yy, u)
                dve.wait_ge(s_dn, u + 1)
                for t in range(TPC):
                    row = y[:, bass.ds(c * TPC + t, 1), :].rearrange("p a d -> p (a d)")
                    ins = v.scalar_tensor_tensor(out=row, in0=ps_y[b][:, t, :], scalar=weights[:, bass.ds(e * NT + c * TPC + t, 1)],
                                                 in1=row, op0=ALU.mult, op1=ALU.add)
                ins.then_inc(s_yy, 1)

            def step(u, i):
                b = i % 2
                dve.wait_ge(s_silu, u + 1)
                wait_past(dve, s_hlo, u, 2)
                v.tensor_tensor(hh[b][:, :], ps_u[b][:, :], sg[b][:, :], ALU.mult).then_inc(s_hh, 1)
                if not (isinstance(u, int) and u == 0):
                    add_up(u - 1, (i - 1) % ROUND)

            dve.wait_ge(s_zero, 1)
            rounds(dve, step, lambda n: add_up(n - 1, ROUND - 1))


def output_phase(nc, a, keep):
    STEPS = 2
    with ExitStack() as ctx:
        def sb(name, shape, dt=F32):
            return ctx.enter_context(nc.sbuf_tensor(name, shape, dt))

        def sem(name):
            return ctx.enter_context(nc.semaphore(name))

        y = keep["y"]
        x2 = sb("x2", [P, 2, TPC, D])
        yn = sb("yn", [P, 2, TPC, D])
        res = sb("res", [P, 2, TPC, D])
        norm = Norm(nc, sb, sem, "p6")
        s_const = sem("p6_const")
        s_in = sem("p6_in")
        s_dve = sem("p6_dve")
        s_yn = sem("p6_yn")
        s_res = sem("p6_res")
        s_out = sem("p6_out")
        x2_dram = a["x2"].rearrange("(c t p) d -> c p t d", t=TPC, p=P)
        out_dram = a["out"].rearrange("a (c t p) d -> c (a p) t d", t=TPC, p=P)
        block = ctx.enter_context(nc.Block())

        def chunks(engine):
            with engine.Fori(0, NCH // 2) as pair:
                for b in range(2):
                    yield pair * 2 + b, b

        @block.sync
        def _(sp):
            for c, b in chunks(sp):
                sp.wait_ge(s_res, c)
                sp.dma_start(x2[:, b, :, :], x2_dram[bass.ds(c, 1)].rearrange("a p t d -> p (a t) d")).then_inc(s_in, 16)

        @block.scalar
        def _(act):
            for c, b in chunks(act):
                act.wait_ge(s_res, c + 1)
                act.dma_start(out_dram[bass.ds(c, 1)].rearrange("a p t d -> p (a t) d"), res[:, b, :, :]).then_inc(s_out, 16)
            act.wait_ge(s_out, 16 * NCH)

        @block.gpsimd
        def _(pool):
            pool.wait_ge(s_const, 1)
            for c, b in chunks(pool):
                norm.root(nc, pool, c)
                pool.wait_ge(s_in, 16 * (c + 1))
                pool.wait_ge(s_out, 16 * c)
                pool.wait_ge(s_yn, c + 1)
                nc.gpsimd.tensor_tensor(res[:, b, :, :], yn[:, b, :, :], x2[:, b, :, :], ALU.add).then_inc(s_res, 1)

        @block.vector
        def _(dve):
            norm.constants().then_inc(s_const, 1)
            dve.wait_ge(s_const, 1)
            for c, b in chunks(dve):
                st = Steps(dve, s_dve, c * STEPS)
                dve.wait_ge(s_res, c)
                norm.rows(dve, st, c, y[:, bass.ds(c * TPC, TPC), :], yn[:, b], s_yn)
                assert st.count == STEPS


def lay_out(inputs):
    import numpy as np

    bf16 = mybir.dt.np(BF16)

    def arr(name):
        return np.ascontiguousarray(inputs[name])

    def cols(x):
        return np.ascontiguousarray(x.reshape(-1, P).T)

    def rows(x):
        return np.ascontiguousarray(np.broadcast_to(x.reshape(1, -1), (P, x.size)))

    half = DH // 2
    freqs = np.exp(-np.arange(half, dtype=np.float32) * np.float32(np.log(10000.0) / half)).astype(np.float32)
    theta = np.arange(T, dtype=np.float32)[:, None] * freqs[None, :]
    cos, sin = np.cos(theta), np.sin(theta)
    shared = np.stack([np.concatenate([arr("L0_ffn_shared_gate_w")[i * NI:(i + 1) * NI],
                                       arr("L0_ffn_shared_up_w")[i * NI:(i + 1) * NI]]) for i in range(2)])
    unit = np.arange(NCH * NE).reshape(-1, P).T
    out = {
        "x": arr("L0_attn_x"), "wq": arr("L0_attn_Wq"), "wk": arr("L0_attn_Wk"), "wv": arr("L0_attn_Wv"),
        "gate_w": arr("L0_attn_gate_w"), "p_w": arr("L0_attn_p_w"), "clock_w": arr("L0_attn_clock_w"),
        "out_w": arr("L0_attn_out_w"), "w1": arr("L0_attn_mlp_w1"), "w2": arr("L0_attn_mlp_w2"),
        "gate_b": cols(arr("L0_attn_gate_b")), "p_b": cols(arr("L0_attn_p_b")),
        "ln1_g": cols(arr("L0_attn_ln1_g")), "ln1_b": cols(arr("L0_attn_ln1_b")),
        "ln2_g": cols(arr("L0_attn_ln2_g")), "ln2_b": cols(arr("L0_attn_ln2_b")),
        "b1": cols(arr("L0_attn_mlp_b1")),
        "clock_b": rows(arr("L0_attn_clock_b")), "out_b": rows(arr("L0_attn_out_b")), "b2": rows(arr("L0_attn_mlp_b2")),
        "score_bias": rows(arr("L0_ffn_e_score_bias")),
        "router_w": np.ascontiguousarray(arr("L0_ffn_router_weight").T),
        "experts_w": np.concatenate([
            np.concatenate([arr("L0_ffn_gate_up_proj").transpose(0, 2, 1).reshape(NE, KT, P, 2 * NI).transpose(0, 2, 1, 3)
                            .reshape(NE, P, -1), arr("L0_ffn_down_proj").transpose(0, 2, 1)], axis=2),
            np.concatenate([shared.transpose(0, 2, 1).reshape(2, KT, P, 2 * NI).transpose(0, 2, 1, 3).reshape(2, P, -1),
                            arr("L0_ffn_shared_down_w").T.reshape(2, NI, D)], axis=2),
            np.zeros((1, P, (KT * 2 + 2) * NI), np.float32)]),
        "rot_c": np.repeat(cos, 2, axis=1).astype(np.float32),
        "rot_s": np.stack([-sin, sin], -1).reshape(T, DH).astype(np.float32),
        "experts": rows(np.arange(NE, dtype=np.float32)),
        "listed": np.stack([np.r_[NE + np.arange(FIXED) % 2, np.full(NCH * NE, FILLER)],
                            np.r_[np.arange(FIXED) // 2, np.zeros(NCH * NE)]])[None].astype(np.uint32),
        "upto": np.triu(np.ones((P, P), np.float32)),
        "places": rows(np.arange(1, NCH * NE + 1, dtype=np.float32)),
        "codes": np.ascontiguousarray(np.stack([unit % NE - FILLER, unit // NE], -1).astype(np.float32)),
        "eye": np.eye(P, dtype=np.float32),
        "eye16": np.eye(P).astype(bf16),
        "mask_q": np.where(np.arange(P)[None, :] > np.arange(P)[:, None], BIG, 0.0).astype(bf16),
        "mask_k": np.where(np.arange(CH + 3 * P)[None, :] - 3 * P < np.arange(P)[:, None], BIG, 0.0).astype(bf16),
        "fold": (np.arange(P)[:, None] % (2 * DH) == np.arange(DH + 1)[None, :]).astype(np.float32),
    }
    return out


def build_kernel(nc, a):
    with ExitStack() as ctx:
        a["x0"] = nc.dram_tensor("x0_scratch", [T, D], F32).ap()
        a["qkt"] = nc.dram_tensor("qkt_scratch", [2 * D, T], F32).ap()
        a["parts"] = nc.dram_tensor("parts_scratch", [2, PARTS, D, T], BF16).ap()
        a["x2"] = nc.dram_tensor("x2_scratch", [T, D], F32).ap()

        region = T * KT * 4
        top = nc.sbuf_usable_end // 256 * 256

        def at(name, shape, dt, start):
            return nc.alloc_sbuf_tensor_at(name, shape, dt, offset=top - start)

        keep = {
            "att": at("att", [P, NT, D], F32, region),
            "v": at("v_all", [P, NT, D], F32, 2 * region),
            "pt": at("pt", [P, KT, T], F32, 3 * region),
            "gt": at("gt", [P, KT, T], F32, 4 * region),
            "comb": at("comb", [P, NE + 3, NT], F32, 2 * region),
            "counts": at("counts", [1, NCH * NE], F32, 2 * region - (NE + 3) * NT * 4),
            "listed": at("unit_list", [1, 2, FIXED + NCH * NE], U32, region + 8192),
            "more_rounds": at("more_rounds", [1, 1], U32, region + 4096),
            "x3h": at("x3h", [P, KT, T], F32R, 3 * region),
            "x3l": at("x3l", [P, KT, T], F32R, 4 * region),
            "y": at("y", [P, NT, D], F32, region),
            "ident": ctx.enter_context(nc.sbuf_tensor("ident", [P, P], F32)),
            "clk": ctx.enter_context(nc.sbuf_tensor("clk", [P, NT, H], F32)),
        }
        with nc.semaphore("k0_ident") as s_ident, nc.Block() as block:
            @block.sync
            def _(sp):
                sp.dma_start(keep["ident"][:, :], a["eye"]).then_inc(s_ident, 16)
                sp.wait_ge(s_ident, 16)
        for phase in (project_phase, stack_phase, attention_phase, mlp_phase, list_phase,
                      expert_phase, output_phase):
            phase(nc, a, keep)


def kernel(**inputs):
    import numpy as np
    import concourse.bacc as bacc
    from concourse.bass_utils import run_bass_kernel_spmd as run

    arrays = lay_out(inputs)
    nc = bacc.Bacc("TRN2", target_bir_lowering=False, num_devices=1)
    a = {name: nc.dram_tensor(f"in_{name}", x.shape, mybir.dt.from_np(x.dtype), kind="ExternalInput").ap()
         for name, x in arrays.items()}
    a["out"] = nc.dram_tensor("out", [1, T, D], F32, kind="ExternalOutput").ap()
    build_kernel(nc, a)
    r = run(nc, [{f"in_{name}": x for name, x in arrays.items()}], core_ids=[0])
    return r.results[0]["out"]
```

```python
from contextlib import ExitStack

import concourse.bass as bass
from concourse import mybir

ALU = mybir.AluOpType
ACT = mybir.ActivationFunctionType
AX = mybir.AxisListType
F32 = mybir.dt.float32
F32R = mybir.dt.float32r
BF16 = mybir.dt.bfloat16
U32 = mybir.dt.uint32

P = 128
T = 4096
D = 256
H = 16
DH = D // H
KT = D // P
CH = 512
NCH = T // CH
TPC = CH // P
NT = T // P
FF = 4 * D
FT = FF // P
NE = 32
NI = 128
TOPK = 6
EPS = 1e-5
QSCALE = 2.0 ** 40
BIG = -3e38
FILLER = NE + 2
FIXED = 2 * NCH
ROUND = 4
SPAN = 8
SPANS = -(-(FIXED + NCH * NE - ROUND) // (ROUND * SPAN))
ROUNDS = 1 + SPANS * SPAN
PARTS = 3
NPROD = 6
Q_PARTS = (0, 0, 1, 1, 0, 2)
K_PARTS = (0, 1, 0, 1, 2, 0)
SROWS = NPROD * DH


class Steps:

    def __init__(self, engine, sem, base=0):
        self.engine, self.sem, self.base, self.count = engine, sem, base, 0

    def step(self, ins):
        self.count += 1
        return ins.then_inc(self.sem, 1)

    def done(self):
        self.engine.wait_ge(self.sem, self.base + self.count)


def by_part(ap):
    return ap.rearrange("(t p) n -> p t n", p=P)


def project_phase(nc, a, keep):
    LN_STEPS = 2
    DVE_STEPS = 2 * LN_STEPS + 8 + KT
    USES = 2 * KT + TPC
    with ExitStack() as ctx:
        def sb(name, shape, dt=F32):
            return ctx.enter_context(nc.sbuf_tensor(name, shape, dt))

        def psum(name, shape):
            return ctx.enter_context(nc.psum_tensor(name, shape, F32))

        def sem(name):
            return ctx.enter_context(nc.semaphore(name))

        wqk = sb("wqk", [P, KT, 2 * D])
        wvc = sb("wvc", [P, KT, D + H])
        wgp = sb("wgp", [P, KT, 2 * D])
        g1 = sb("g1", [P, KT])
        b1 = sb("b1", [P, KT])
        gpb = sb("gpb", [P, 2 * KT])
        rot_c = sb("rot_c", [P, NT, DH])
        rot_s = sb("rot_s", [P, NT, DH])
        neghalf = sb("neghalf", [P, TPC])
        ones = sb("ones_row", [P, CH])
        xin = sb("xin", [P, TPC, D])
        x0 = sb("x0", [P, TPC, D])
        xn = sb("xn", [P, TPC, D])
        stats = sb("stats", [P, TPC, 6])
        mv = sb("mv", [P, TPC, 2])
        veps = sb("veps", [P, TPC])
        rstd = sb("rstd", [P, TPC])
        xnt = sb("xnt", [P, KT, CH])
        ssq = sb("ssq", [P, TPC, 2 * H])
        nrm = sb("nrm", [P, TPC, 2 * H])
        rnrm = sb("rnrm", [P, TPC, 2 * H])
        qkr = sb("qkr", [P, TPC, 2 * D])
        qkt = sb("qkt", [P, 2 * KT, CH])
        gx = sb("gx", [P, KT, CH])
        ga = sb("ga", [P, KT, CH])
        gl = sb("gl", [P, KT, CH])
        gd = sb("gd", [P, KT, CH])
        gsum = sb("gsum", [P, KT, CH])
        spare = sb("spare", [P, 1])
        epst = sb("epst", [P, TPC])
        carry = sb("carry", [P, KT])
        sq, qkn, rc, rs = (keep["p1_wide"][:, i] for i in range(4))

        ps_xt = psum("ps_xt", [P, KT, CH])
        ps_qk = psum("ps_qk", [P, TPC, 2 * D])
        ps_w = psum("ps_w", [P, 2, CH])

        s_const = sem("p1_const")
        s_x = sem("p1_x")
        s_dve = sem("p1_dve")
        s_var = sem("p1_var")
        s_veps = sem("p1_veps")
        s_rstd = sem("p1_rstd")
        s_x0 = sem("p1_x0")
        s_x0out = sem("p1_x0out")
        s_xn = sem("p1_xn")
        s_xt = sem("p1_xt")
        s_xnt = sem("p1_xnt")
        s_qk = sem("p1_qk")
        s_w = sem("p1_w")
        s_wr = sem("p1_wr")
        s_sq = sem("p1_sq")
        s_ssq = sem("p1_ssq")
        s_nrm = sem("p1_nrm")
        s_qkn = sem("p1_qkn")
        s_rs = sem("p1_rs")
        s_qkr = sem("p1_qkr")
        s_rt = sem("p1_rt")
        s_qkt = sem("p1_qkt")
        s_qktout = sem("p1_qktout")
        s_abs = sem("p1_abs")
        s_exp = sem("p1_exp")
        s_ln = sem("p1_ln")
        s_gclip = sem("p1_gclip")
        s_gexp = sem("p1_gexp")
        NLOADS = 12

        x_dram = a["x"].rearrange("a (c t p) d -> c (a p) t d", t=TPC, p=P)
        x0_dram = a["x0"].rearrange("(c t p) d -> c p t d", t=TPC, p=P)
        qkt_dram = a["qkt"].rearrange("(m p) (c n) -> c p m n", p=P, n=CH)

        def chunks(engine, body):
            body(0, False, True)
            with engine.Fori(1, NCH - 1) as c:
                body(c, True, True)
            body(NCH - 1, True, False)

        block = ctx.enter_context(nc.Block())

        @block.sync
        def _(sp):
            sp.dma_start(xin[:, :, :], x_dram[0]).then_inc(s_x, 16)
            sp.dma_start(wqk[:, :, 0:D], by_part(a["wq"])).then_inc(s_const, 16)
            sp.dma_start(wqk[:, :, D:], by_part(a["wk"])).then_inc(s_const, 16)
            sp.dma_start(wvc[:, :, 0:D], by_part(a["wv"])).then_inc(s_const, 16)
            sp.dma_start(wvc[:, :, D:], by_part(a["clock_w"])).then_inc(s_const, 16)
            sp.dma_start(wgp[:, :, 0:D], by_part(a["gate_w"])).then_inc(s_const, 16)
            sp.dma_start(wgp[:, :, D:], by_part(a["p_w"])).then_inc(s_const, 16)
            sp.dma_start(g1[:, :], a["ln1_g"]).then_inc(s_const, 16)
            sp.dma_start(b1[:, :], a["ln1_b"]).then_inc(s_const, 16)
            sp.dma_start(gpb[:, 0:KT], a["gate_b"]).then_inc(s_const, 16)
            sp.dma_start(gpb[:, KT:], a["p_b"]).then_inc(s_const, 16)
            sp.dma_start(rot_c[:, :, :], by_part(a["rot_c"])).then_inc(s_const, 16)
            sp.dma_start(rot_s[:, :, :], by_part(a["rot_s"])).then_inc(s_const, 16)

            def body(c, before, after):
                sp.wait_ge(s_x0, c + 1)
                sp.dma_start(x0_dram[bass.ds(c, 1)].rearrange("a p t d -> p (a t) d"), x0[:, :, :]).then_inc(s_x0out, 16)
                if after:
                    sp.dma_start(xin[:, :, :], x_dram[bass.ds(c + 1, 1)].rearrange("a p t d -> p (a t) d")).then_inc(s_x, 16)

            chunks(sp, body)
            sp.wait_ge(s_x0out, 16 * NCH)
            sp.wait_ge(s_qktout, 16 * NCH)

        @block.vector
        def _(dve):
            v = nc.vector
            v.memset(neghalf[:, :], -0.5).then_inc(s_dve, 1)
            v.memset(ones[:, :], 1.0).then_inc(s_dve, 1)
            v.memset(epst[:, :], EPS).then_inc(s_dve, 1)
            v.memset(carry[:, :], 0.0).then_inc(s_dve, 1)

            def layernorm(st, c, src, out, nth, out_sem):
                for t in range(TPC):
                    ins = v.bn_stats(stats[:, t, :], src[:, t, :])
                st.step(ins)
                st.done()
                st.step(v.memset(spare[:, :], 0.0))
                for t in range(TPC):
                    ins = v.bn_aggr(mv[:, t, :], stats[:, t, :])
                ins.then_inc(s_var, 1)
                dve.wait_ge(s_rstd, 2 * c + nth)
                for t in range(TPC):
                    ins = v.tensor_scalar(out[:, t, :], src[:, t, :], mv[:, t, 0:1], rstd[:, t:t + 1],
                                          ALU.subtract, ALU.mult)
                ins.then_inc(out_sem, 1)

            def first_norm(st, c):
                dve.wait_ge(s_x, 16 * (c + 1))
                dve.wait_ge(s_x0out, 16 * c)
                dve.wait_ge(s_xn, c)
                layernorm(st, c, xin, x0, 1, s_x0)

            def second_norm(st, c):
                dve.wait_ge(s_x0, c + 1)
                dve.wait_ge(s_xt, c)
                layernorm(st, c, x0, xn, 2, s_xn)

            def by_head(x):
                return x.rearrange("p t (h d) -> p (t h) d", d=DH)

            def spread(x):
                return x[:, :, :].rearrange("p t (h a) -> p (t h) a", a=1).to_broadcast([P, TPC * 2 * H, DH])

            def body(c, before, after):
                st = Steps(dve, s_dve, c * DVE_STEPS + 4 + 2 * LN_STEPS)

                def step(ins):
                    st.step(ins)
                    st.done()

                if after:
                    first_norm(st, c + 1)
                dve.wait_ge(s_sq, TPC * (c + 1))
                v.tensor_reduce(ssq[:, :, :].rearrange("p t h -> p (t h)"), by_head(sq), AX.X, ALU.add).then_inc(s_ssq, 1)
                if after:
                    second_norm(st, c + 1)
                dve.wait_ge(s_nrm, c + 1)
                step(v.tensor_scalar(nrm[:, :, :], nrm[:, :, :], 1e-12, None, ALU.max))
                step(v.reciprocal(rnrm[:, :, :], nrm[:, :, :]))
                dve.wait_ge(s_rs, c)
                v.tensor_tensor(by_head(qkn), by_head(ps_qk), spread(rnrm), ALU.mult).then_inc(s_qkn, 1)
                dve.wait_ge(s_qkn, c + 1)
                for t in range(TPC):
                    ins = v.tensor_tensor(rc[:, t, :].rearrange("p (h d) -> p h d", d=DH),
                                          qkn[:, t, :].rearrange("p (h d) -> p h d", d=DH),
                                          rot_c[:, bass.ds(c * TPC + t, 1), :].to_broadcast([P, 2 * H, DH]), ALU.mult)
                st.step(ins)

                dve.wait_ge(s_ln, c + 1)
                step(v.tensor_scalar(gd[:, :, :], ga[:, :, :], 1.0, -1.0, ALU.add, ALU.add))
                step(v.tensor_tensor(gd[:, :, :], ga[:, :, :], gd[:, :, :], ALU.subtract))
                step(v.tensor_tensor(gd[:, :, :], gd[:, :, :], gl[:, :, :], ALU.add))
                step(v.scalar_tensor_tensor(out=gd[:, :, :], in0=gx[:, :, :], scalar=0.0, in1=gd[:, :, :],
                                            op0=ALU.max, op1=ALU.add))
                dve.wait_ge(s_gexp, c)
                for m in range(KT):
                    st.step(v.tensor_tensor_scan(gsum[:, m, :], ones[:, :], gd[:, m, :], carry[:, m:m + 1],
                                                 ALU.mult, ALU.subtract))
                st.done()
                step(v.tensor_copy(carry[:, :], gsum[:, :, CH - 1]))
                v.tensor_scalar(gsum[:, :, :], gsum[:, :, :], -60.0, 50.0, ALU.max, ALU.min).then_inc(s_gclip, 1)

                dve.wait_ge(s_rs, c + 1)
                dve.wait_ge(s_rt, TPC * c)
                v.tensor_tensor(qkr[:, :, :], rc, rs, ALU.add).then_inc(s_qkr, 1)
                if after:
                    assert st.count == DVE_STEPS, st.count

            st = Steps(dve, s_dve, 4)
            first_norm(st, 0)
            second_norm(st, 0)
            dve.wait_ge(s_const, 16 * NLOADS)
            chunks(dve, body)

        @block.gpsimd
        def _(pool):
            g = nc.gpsimd
            pool.wait_ge(s_dve, 4)

            def root(nth):
                pool.wait_ge(s_var, nth + 1)
                g.tensor_tensor(veps[:, :], mv[:, :, 1], epst[:, :], ALU.add).then_inc(s_veps, 1)
                pool.wait_ge(s_veps, nth + 1)
                g.tensor_tensor(rstd[:, :], veps[:, :], neghalf[:, :], ALU.pow).then_inc(s_rstd, 1)

            def body(c, before, after):
                if after:
                    root(2 * (c + 1))
                    root(2 * (c + 1) + 1)
                pool.wait_ge(s_qkn, c + 1)
                pool.wait_ge(s_qkr, c)
                for t in range(TPC):
                    src = qkn[:, t, :].rearrange("p (h d two) -> p h d two", d=DH // 2, two=2)
                    dst = rs[:, t, :].rearrange("p (h d two) -> p h d two", d=DH // 2, two=2)
                    rot = rot_s[:, bass.ds(c * TPC + t, 1), :].rearrange("p a (d two) -> p a d two", two=2)
                    for i in range(2):
                        ins = g.tensor_tensor(dst[:, :, :, i], src[:, :, :, 1 - i],
                                              rot[:, :, :, i].to_broadcast([P, 2 * H, DH // 2]), ALU.mult)
                ins.then_inc(s_rs, 1)

            root(0)
            root(1)
            pool.wait_ge(s_const, 16 * NLOADS)
            chunks(pool, body)

        @block.scalar
        def _(act):
            s = nc.scalar
            act.wait_ge(s_const, 16 * NLOADS)

            def turned_in(c):
                act.wait_ge(s_xt, c + 1)
                act.wait_ge(s_w, USES * c)
                act.wait_ge(s_qk, TPC * c)
                for m in range(KT):
                    ins = s.activation(xnt[:, m, :], ps_xt[:, m, :], ACT.Identity, bias=b1[:, m:m + 1],
                                       scale=g1[:, m:m + 1])
                ins.then_inc(s_xnt, 1)

            def turned_back(c):
                act.wait_ge(s_qktout, 16 * c)
                for t in range(TPC):
                    act.wait_ge(s_rt, TPC * c + t + 1)
                    s.activation(qkt[:, :, t * P:(t + 1) * P], ps_xt[:, t % 2, :].rearrange("p (m n) -> p m n", n=P),
                                 ACT.Copy).then_inc(s_qkt, 1)
                act.wait_ge(s_qkt, TPC * (c + 1))
                act.dma_start(qkt_dram[bass.ds(c, 1)].rearrange("a p m n -> p (a m) n"), qkt[:, :, :]).then_inc(s_qktout, 16)

            def gates(c):
                act.wait_ge(s_gclip, c + 1)
                s.activation(keep["gt"][:, :, bass.ds(c * CH, CH)], gsum[:, :, :], ACT.Exp).then_inc(s_gexp, 1)

            def body(c, before, after):
                for m in range(KT):
                    act.wait_ge(s_w, USES * c + m + 1)
                    s.activation(keep["pt"][:, m, bass.ds(c * CH, CH)], ps_w[:, m % 2, :], ACT.Identity,
                                 bias=gpb[:, KT + m:KT + m + 1]).then_inc(s_wr, 1)
                act.wait_ge(s_gclip, c)
                for m in range(KT):
                    act.wait_ge(s_w, USES * c + KT + m + 1)
                    s.activation(gx[:, m, :], ps_w[:, (KT + m) % 2, :], ACT.Identity, bias=gpb[:, m:m + 1]).then_inc(s_wr, 1)
                act.wait_ge(s_wr, USES * c + 2 * KT)
                s.activation(ga[:, :, :], gx[:, :, :], ACT.Abs).then_inc(s_abs, 1)
                act.wait_ge(s_abs, c + 1)
                s.activation(ga[:, :, :], ga[:, :, :], ACT.Exp, scale=-1.0).then_inc(s_exp, 1)
                if before:
                    gates(c - 1)
                act.wait_ge(s_ssq, c)
                for t in range(TPC):
                    act.wait_ge(s_qk, TPC * c + t + 1)
                    s.activation(sq[:, t, :], ps_qk[:, t, :], ACT.Square).then_inc(s_sq, 1)
                act.wait_ge(s_exp, c + 1)
                s.activation(gl[:, :, :], ga[:, :, :], ACT.Ln, bias=1.0).then_inc(s_ln, 1)
                act.wait_ge(s_qkn, c)
                act.wait_ge(s_ssq, c + 1)
                s.activation(nrm[:, :, :], ssq[:, :, :], ACT.Sqrt).then_inc(s_nrm, 1)
                if before:
                    turned_back(c - 1)
                for t in range(TPC):
                    use = 2 * KT + t
                    act.wait_ge(s_w, USES * c + use + 1)
                    s.activation(keep["v"][:, bass.ds(c * TPC + t, 1), :].rearrange("p a d -> p (a d)"),
                                 ps_w[:, use % 2, 0:D], ACT.Copy)
                    s.activation(keep["clk"][:, bass.ds(c * TPC + t, 1), :].rearrange("p a h -> p (a h)"),
                                 ps_w[:, use % 2, D:D + H], ACT.Copy).then_inc(s_wr, 1)
                if after:
                    turned_in(c + 1)

            turned_in(0)
            chunks(act, body)
            gates(NCH - 1)
            turned_back(NCH - 1)

        @block.tensor
        def _(pe):
            m_ = nc.tensor
            pe.wait_ge(s_const, 16 * NLOADS)

            def turn_in(c):
                pe.wait_ge(s_xn, c + 1)
                if not isinstance(c, int) or c >= 2:
                    pe.wait_ge(s_qkt, TPC * (c - 1))
                for t in range(TPC):
                    for m in range(KT):
                        ins = m_.transpose(ps_xt[:, m, t * P:(t + 1) * P], xn[:, t, m * P:(m + 1) * P],
                                           keep["ident"][:, :])
                ins.then_inc(s_xt, 1)

            def turn_back(c):
                pe.wait_ge(s_qkr, c + 1)
                for t in range(TPC):
                    if t >= 2:
                        pe.wait_ge(s_qkt, TPC * c + t - 1)
                    for m in range(2 * KT):
                        ins = m_.transpose(ps_xt[:, t % 2, m * P:(m + 1) * P], qkr[:, t, m * P:(m + 1) * P],
                                           keep["ident"][:, :])
                    ins.then_inc(s_rt, 1)

            def bank(c, use):
                if use >= 2:
                    pe.wait_ge(s_wr, USES * c + use - 1)
                elif not (isinstance(c, int) and c == 0):
                    pe.wait_ge(s_wr, USES * c + use - 1)
                return ps_w[:, use % 2, :]

            def body(c, before, after):
                pe.wait_ge(s_xnt, c + 1)
                for m in range(2 * KT):
                    out = bank(c, m)
                    col = (KT + m if m < KT else m - KT) * P
                    for k in range(KT):
                        ins = m_.matmul(out, wgp[:, k, col:col + P], xnt[:, k, :], start=(k == 0), stop=(k == KT - 1))
                    ins.then_inc(s_w, 1)
                pe.wait_ge(s_qkn, c)
                for t in range(TPC):
                    tok = slice(t * P, (t + 1) * P)
                    for k in range(KT):
                        ins = m_.matmul(ps_qk[:, t, :], xnt[:, k, tok], wqk[:, k, :], start=(k == 0), stop=(k == KT - 1))
                    ins.then_inc(s_qk, 1)
                if before:
                    turn_back(c - 1)
                for t in range(TPC):
                    tok = slice(t * P, (t + 1) * P)
                    out = bank(c, 2 * KT + t)
                    for k in range(KT):
                        ins = m_.matmul(out[:, 0:D + H], xnt[:, k, tok], wvc[:, k, :], start=(k == 0), stop=(k == KT - 1))
                    ins.then_inc(s_w, 1)
                if after:
                    turn_in(c + 1)

            turn_in(0)
            chunks(pe, body)
            turn_back(NCH - 1)


def stack_phase(nc, a, keep):
    CLOCK_STEPS = 5
    with ExitStack() as ctx:
        def sb(name, shape, dt=F32):
            return ctx.enter_context(nc.sbuf_tensor(name, shape, dt))

        def sem(name):
            return ctx.enter_context(nc.semaphore(name))

        qk = sb("qk_in", [P, 2, 2, CH])
        clockb = sb("clockb", [P, H])
        cabs = sb("cabs", [P, NT, H])
        cexp = sb("cexp", [P, NT, H])
        cln = sb("cln", [P, NT, H])
        clow = sb("clow", [P, NT, H])
        stage = sb("stage", [P, 2, TPC, P])
        npmax = sb("npmax", [P, KT])
        pe_x = sb("pe_x", [P, 2, CH])
        pexp = sb("pexp", [P, 2, CH])
        pcs = sb("pcs", [P, CH])
        pcarry = sb("pcarry", [P, KT])
        onesr = sb("onesr", [P, CH])
        pcs8 = sb("pcs8", [P, 2, CH])
        ge_pcs = sb("ge_pcs", [P, CH])
        rec = sb("rec", [P, 2, CH])
        num = sb("num", [P, CH])
        rge = sb("rge", [P, CH])
        ge8 = sb("ge8", [P, CH])
        fac = sb("fac", [P, 2, CH])
        full = sb("full", [P, 2, CH])
        rest = sb("rest", [P, 2, CH])
        parts = sb("parts", [P, 2, 2, PARTS, CH], BF16)
        ps_ct = ctx.enter_context(nc.psum_tensor("ps_ct", [P, 2, CH], F32))

        s_in = sem("p2_in")
        s_clkin = sem("p2_clkin")
        s_clkb = sem("p2_clkb")
        s_cabs = sem("p2_cabs")
        s_dve = sem("p2_dve")
        s_clk = sem("p2_clk")
        s_stage = sem("p2_stage")
        s_ct = sem("p2_ct")
        s_max = sem("p2_max")
        s_pexp = sem("p2_pexp")
        s_scan = sem("p2_scan")
        s_carry = sem("p2_carry")
        s_prod = sem("p2_prod")
        s_div = sem("p2_div")
        s_num = sem("p2_num")
        s_rec = sem("p2_rec")
        s_fac = sem("p2_fac")
        s_pe = sem("p2_pe")
        s_hi = sem("p2_hi")
        s_rest = sem("p2_rest")
        s_mid = sem("p2_mid")
        s_lo = sem("p2_lo")
        s_full = sem("p2_full")
        s_out = [sem(f"p2_out{b}") for b in range(2)]

        qkt_dram = a["qkt"].rearrange("(w m p) (c n) -> m c p w n", w=2, p=P, n=CH)
        parts_dram = a["parts"].rearrange("w r (m p) (c n) -> m c p (w r) n", p=P, n=CH)
        pt, gt, clk = keep["pt"], keep["gt"], keep["clk"]
        block = ctx.enter_context(nc.Block())

        def units(engine):
            for m in range(KT):
                with engine.Fori(0, NCH // 2) as pair:
                    for b in range(2):
                        yield m, pair * 2 + b, b, pair * 2 + (m * NCH + b)

        def in_turn(engine, both):
            for m in range(KT):
                def unit(c, b):
                    return m, c, b, c + m * NCH

                both(unit(0, 0), None)
                with engine.Fori(0, NCH // 2 - 1) as pair:
                    for b in (1, 0):
                        both(unit(pair * 2 + (2 - b), b), unit(pair * 2 + (1 - b), 1 - b))
                both(unit(NCH - 1, 1), unit(NCH - 2, 0))
                both(None, unit(NCH - 1, 1))

        def staggered(engine, first, second):
            def both(new, old):
                if new:
                    first(*new)
                if old:
                    second(*old)

            in_turn(engine, both)

        @block.sync
        def _(sp):
            sp.dma_start(clockb[:, :], a["clock_b"]).then_inc(s_clkin, 16)
            for m, c, b, u in units(sp):
                sp.wait_ge(s_full, u)
                sp.dma_start(qk[:, b, :, :], qkt_dram[m, bass.ds(c, 1)].rearrange("a p w n -> p (a w) n")).then_inc(s_in, 16)
            for b in range(2):
                sp.wait_ge(s_out[b], 16 * KT * NCH // 2)

        @block.scalar
        def _(act):
            s = nc.scalar
            act.wait_ge(s_clkb, 1)
            s.activation(cabs[:, :, :], clk[:, :, :], ACT.Abs).then_inc(s_cabs, 1)
            act.wait_ge(s_cabs, 1)
            s.activation(cexp[:, :, :], cabs[:, :, :], ACT.Exp, scale=-1.0).then_inc(s_cabs, 1)
            act.wait_ge(s_cabs, 2)
            s.activation(cln[:, :, :], cexp[:, :, :], ACT.Ln, bias=1.0).then_inc(s_cabs, 1)
            act.wait_ge(s_max, 1)

            def first(m, c, b, u):
                act.wait_ge(s_pe, u)
                s.activation(pe_x[:, b, :], pt[:, m, bass.ds(c * CH, CH)], ACT.Exp,
                             bias=npmax[:, m:m + 1]).then_inc(s_pexp, 1)

            def second(m, c, b, u):
                act.wait_ge(s_out[b], (16 // 2) * (u - b))
                act.wait_ge(s_full, u + 1)
                s.activation(parts[:, b, :, 0, :], full[:, :, :], ACT.Copy).then_inc(s_hi, 1)
                act.wait_ge(s_rest, u + 1)
                s.activation(parts[:, b, :, 1, :], rest[:, :, :], ACT.Copy).then_inc(s_mid, 1)
                act.wait_ge(s_lo, u + 1)
                act.dma_start(parts_dram[m, bass.ds(c, 1)].rearrange("a p r n -> p (a r) n"),
                              parts[:, b].rearrange("p w r n -> p (w r) n")).then_inc(s_out[b], 16)

            staggered(act, first, second)

        @block.gpsimd
        def _(pool):
            g = nc.gpsimd
            pool.wait_ge(s_clk, 1)

            def first(m, c, b, u):
                pool.wait_ge(s_ct, u)
                heads = clk[:, bass.ds(c * TPC, TPC), m * H // KT:(m + 1) * H // KT]
                g.tensor_copy(stage[:, b, :, :].rearrange("p t (h d) -> p t h d", d=DH),
                                      heads.rearrange("p t (h a) -> p t h a", a=1).to_broadcast([P, TPC, H // KT, DH])
                                      ).then_inc(s_stage, 1)

            def numerator(m, c, b, u):
                pool.wait_ge(s_div, u + 1)
                g.tensor_tensor(num[:, :], gt[:, m, bass.ds(c * CH, CH)], ge8[:, :], ALU.mult).then_inc(s_num, 1)

            def second(m, c, b, u):
                pool.wait_ge(s_rec, u + 1)
                g.tensor_tensor(rge[:, :], rec[:, b, :], pcs8[:, b, :], ALU.mult).then_inc(s_num, 1)
                pool.wait_ge(s_full, u)
                pool.wait_ge(s_num, 2 * u + 1)
                g.tensor_tensor(fac[:, 0, :], num[:, :], rec[:, b, :], ALU.mult)
                pool.wait_ge(s_num, 2 * u + 2)
                g.tensor_tensor(fac[:, 1, :], rge[:, :], pexp[:, b, :], ALU.mult).then_inc(s_fac, 1)

            def both(new, old):
                if new:
                    first(*new)
                if old:
                    second(*old)
                if new:
                    pool.wait_ge(s_fac, new[3])
                    numerator(*new)

            in_turn(pool, both)

        @block.tensor
        def _(pe):
            for m, c, b, u in units(pe):
                pe.wait_ge(s_stage, u + 1)
                pe.wait_ge(s_pe, u)
                for t in range(TPC):
                    ins = nc.tensor.transpose(ps_ct[:, b, t * P:(t + 1) * P], stage[:, b, t, :], keep["ident"][:, :])
                ins.then_inc(s_ct, 1)

        @block.vector
        def _(dve):
            v = nc.vector
            dve.wait_ge(s_clkin, 16)
            v.tensor_tensor(clk[:, :, :], clk[:, :, :],
                            clockb[:, :].rearrange("p (a h) -> p a h", a=1).to_broadcast([P, NT, H]), ALU.add).then_inc(s_clkb, 1)
            for m in range(KT):
                ins = v.tensor_reduce(npmax[:, m:m + 1], pt[:, m, :], AX.X, ALU.max, negate=True)
            ins.then_inc(s_max, 1)
            v.memset(onesr[:, :], 1.0)
            v.memset(pcarry[:, :], 0.0)
            st = Steps(dve, s_dve)
            dve.wait_ge(s_cabs, 3)
            st.step(v.tensor_scalar(clow[:, :, :], cexp[:, :, :], 1.0, -1.0, ALU.add, ALU.add))
            st.done()
            st.step(v.scalar_tensor_tensor(out=cln[:, :, :], in0=clow[:, :, :], scalar=0.0, in1=cln[:, :, :],
                                           op0=ALU.is_gt, op1=ALU.mult))
            st.done()
            st.step(v.tensor_tensor(clow[:, :, :], cexp[:, :, :], clow[:, :, :], ALU.subtract))
            st.done()
            st.step(v.tensor_tensor(cln[:, :, :], cln[:, :, :], clow[:, :, :], ALU.add))
            st.done()
            v.scalar_tensor_tensor(out=clk[:, :, :], in0=clk[:, :, :], scalar=0.0, in1=cln[:, :, :],
                                   op0=ALU.max, op1=ALU.add).then_inc(s_clk, 1)
            assert st.count == CLOCK_STEPS - 1

            def factors(m, c, b, u):
                def summands():
                    dve.wait_ge(s_pexp, u + 1)
                    dve.wait_ge(s_ct, u + 1)
                    if not (isinstance(u, int) and u == 0):
                        dve.wait_ge(s_fac, u - 1)
                    v.tensor_tensor(pexp[:, b, :], pe_x[:, b, :], ps_ct[:, b, :], ALU.mult).then_inc(s_pe, 1)

                def sums():
                    dve.wait_ge(s_pe, u + 1)
                    dve.wait_ge(s_carry, u)
                    v.tensor_tensor_scan(pcs[:, :], onesr[:, :], pexp[:, b, :], pcarry[:, m:m + 1], ALU.mult,
                                         ALU.add).then_inc(s_scan, 1)

                def divisors():
                    dve.wait_ge(s_scan, u + 1)
                    v.tensor_copy(pcarry[:, m:m + 1], pcs[:, CH - 1:CH]).then_inc(s_carry, 1)
                    v.tensor_scalar(pcs8[:, b, :], pcs[:, :], 1e-8, 1.0 / QSCALE, ALU.add, ALU.mult)
                    v.tensor_scalar(ge8[:, :], gt[:, m, bass.ds(c * CH, CH)], 1e-8, None, ALU.add).then_inc(s_div, 1)

                def inverse():
                    dve.wait_ge(s_div, u + 1)
                    v.tensor_tensor(ge_pcs[:, :], ge8[:, :], pcs8[:, b, :], ALU.mult).then_inc(s_prod, 1)
                    dve.wait_ge(s_prod, u + 1)
                    v.reciprocal(rec[:, b, :], ge_pcs[:, :]).then_inc(s_rec, 1)

                return summands, sums, divisors, inverse

            def split(m, c, b, u):
                def scale():
                    dve.wait_ge(s_in, 16 * (u + 1))
                    dve.wait_ge(s_fac, u + 1)
                    v.tensor_tensor(full[:, :, :], qk[:, b, :, :], fac[:, :, :], ALU.mult).then_inc(s_full, 1)

                def middle():
                    dve.wait_ge(s_hi, u + 1)
                    v.tensor_tensor(rest[:, :, :], full[:, :, :], parts[:, b, :, 0, :], ALU.subtract).then_inc(s_rest, 1)

                def low():
                    dve.wait_ge(s_mid, u + 1)
                    v.tensor_tensor(parts[:, b, :, 2, :], rest[:, :, :], parts[:, b, :, 1, :], ALU.subtract).then_inc(s_lo, 1)

                return scale, middle, low

            def both(new, old):
                summands, sums, divisors, inverse = factors(*new) if new else (None,) * 4
                scale, middle, low = split(*old) if old else (None,) * 3
                for piece in (summands, sums, scale, divisors, middle, inverse, low):
                    if piece:
                        piece()

            in_turn(dve, both)


def attention_phase(nc, a, keep):
    QUADS = [(c, g) for c in range(NCH) for g in range(c + 1)]
    NQ = len(QUADS)
    MUNITS = [(i, j) for i in range(NT) for j in range(i // TPC + 1)]
    assert len(MUNITS) == NQ * TPC
    NM = len(MUNITS)
    MRING = 3
    VW = 2 * DH
    with ExitStack() as ctx:
        def sb(name, shape, dt=F32):
            return ctx.enter_context(nc.sbuf_tensor(name, shape, dt))

        def psum(name, shape):
            return ctx.enter_context(nc.psum_tensor(name, shape, F32))

        def sem(name):
            return ctx.enter_context(nc.semaphore(name))

        qs = [sb(f"qs{b}", [P, T], BF16) for b in range(2)]
        ks = [sb(f"ks{b}", [P, T], BF16) for b in range(2)]
        vs = [sb(f"vs{b}", [P, NT, VW]) for b in range(2)]
        fold = sb("fold", [P, DH + 1])
        ident16 = sb("ident16", [P, P], BF16)
        mask_q = sb("mask_q", [P, P], BF16)
        mask_k = sb("mask_k", [P, CH + 3 * P], BF16)
        ex = [sb(f"ex{i}", [P, TPC, CH]) for i in range(3)]
        maxes = sb("maxes", [P, NM])
        nmax = sb("nmax", [P, NT])
        nrest = sb("nrest", [P, NT])
        nparts = sb("nparts", [P, PARTS, NT], BF16)
        nrows = sb("nrows", [PARTS * NT, P], BF16)
        osb = sb("osb", [P, 2, CH])
        rden = sb("rden", [P, TPC])

        ps_s = [psum(f"ps_s{i}", [P, 2, CH]) for i in range(2)]
        ps_m = [psum(f"ps_m{i}", [P, CH]) for i in range(MRING)]
        ps_o = psum("ps_o", [P, CH])

        s_const = sem("p3_const")
        s_ones = sem("p3_ones")
        s_load = sem("p3_load")
        s_vs = sem("p3_vs")
        s_mm = sem("p3_mm")
        s_mr = sem("p3_mr")
        s_st = sem("p3_st")
        s_ex = sem("p3_ex")
        s_pv = sem("p3_pv")
        s_osb = sem("p3_osb")
        s_dve = sem("p3_dve")
        s_np = sem("p3_np")
        s_nload = sem("p3_nload")
        NLOADS = 4
        parts = a["parts"].rearrange("w r (h d) n -> w r h d n", d=DH)
        att, v_all = keep["att"], keep["v"]

        MFROM, MTO = 5, NQ - 4

        def units_by(q):
            return min(NM, max(0, -(-NM * (q + 1 - MFROM) // (MTO - MFROM))))

        def plan(more):
            for q in range(NQ + 2):
                units = range(units_by(q - 1), units_by(q)) if more else []
                if q < NQ:
                    for half in range(2):
                        yield "scores", (q, half)
                        for u in units[2 * half:2 * half + 2]:
                            yield "unit", u
                if 1 <= q <= NQ:
                    yield "product", q - 1
                for u in units[4:]:
                    yield "unit", u
                if q == MTO + 1 and more:
                    yield "turn", 0
                if 2 <= q and QUADS[q - 2][0] == QUADS[q - 2][1]:
                    yield "fold", QUADS[q - 2][0]

        FIRST = NM + 1
        def uses(more):
            return [x for x in plan(more) if x[0] in ("unit", "turn", "fold")]

        NUSE = len(uses(True))
        assert NUSE == NM + NCH + 1 and NUSE % MRING == 0

        def use_of(h, more, what, n):
            return FIRST + h * NUSE + uses(more).index((what, n))

        MAX_STEPS = NCH + 3
        NLOAD = 2 * NPROD

        block = ctx.enter_context(nc.Block())

        def heads(engine):
            with engine.Fori(0, H // 2 - 1) as pair:
                for b in range(2):
                    yield pair * 2 + b, b, True
            yield H - 2, 0, True
            yield H - 1, 1, False

        @block.sync
        def _(sp):
            sp.dma_start(ident16[:, :], a["eye16"]).then_inc(s_const, 16)
            sp.dma_start(mask_q[:, :], a["mask_q"]).then_inc(s_const, 16)
            sp.dma_start(mask_k[:, :], a["mask_k"]).then_inc(s_const, 16)
            sp.dma_start(fold[:, :], a["fold"]).then_inc(s_const, 16)

            def load(h, b):
                for w, (which, to) in enumerate(((Q_PARTS, qs[b]), (K_PARTS, ks[b]))):
                    for row, part in enumerate(which):
                        sp.dma_start(to[row * DH:(row + 1) * DH, :],
                                     parts[w, part, bass.ds(h, 1)].rearrange("a d n -> (a d) n")).then_inc(s_load, 16)

            def rows_in(b, turned):
                sp.wait_ge(s_mr, turned)
                for r in range(PARTS):
                    sp.dma_start(qs[b][SROWS + r:SROWS + r + 1, :].rearrange("a (t n) -> a t n", n=P),
                                 nrows[r * NT:(r + 1) * NT, :]).then_inc(s_nload, 16)

            load(0, 0)
            rows_in(0, FIRST)
            for h, b, more in heads(sp):
                if more:
                    sp.wait_ge(s_pv, NQ * h)
                    load(h + 1, 1 - b)
                    rows_in(1 - b, use_of(h, True, "turn", 0) + 1)

        @block.gpsimd
        def _(pool):
            g = nc.gpsimd
            for b in range(2):
                g.memset(vs[b][:, :, DH:DH + 1], 1.0)
                g.memset(vs[b][:, :, DH + 1:], 0.0)

            def stage(h, b):
                g.tensor_copy(vs[b][:, :, 0:DH], v_all[:, :, bass.ds(h * DH, DH)]).then_inc(s_vs, 1)

            stage(0, 0)
            for h, b, more in heads(pool):
                if more:
                    pool.wait_ge(s_pv, NQ * h)
                    stage(h + 1, 1 - b)

        def osb_out(act, h, q, more):
            c = QUADS[q][0]
            act.wait_ge(s_pv, NQ * h + q + 1)
            act.wait_ge(s_mm, use_of(h, more, "fold", c - 2) + 1 if c >= 2 else FIRST + h * NUSE)
            nc.scalar.activation(osb[:, c % 2, :], ps_o[:, :], ACT.Copy).then_inc(s_osb, 1)

        @block.scalar
        def _(act):
            s = nc.scalar
            for h, b, more in heads(act):
                for q, (c, g) in enumerate(QUADS):
                    if q >= len(ex):
                        act.wait_ge(s_pv, NQ * h + q - len(ex) + 1)
                    else:
                        act.wait_ge(s_pv, NQ * h)
                    e = ex[q % len(ex)]
                    for half in range(2):
                        act.wait_ge(s_st, 2 * NQ * h + 2 * q + half + 1)
                        if g < c or c == 0:
                            ins = s.activation(e[:, 2 * half:2 * half + 2, :], ps_s[half][:, :, :], ACT.Exp,
                                               scale=DH ** -0.5 / QSCALE)
                        else:
                            for i in range(2):
                                j = 2 * half + i
                                ins = s.activation(e[:, j, j * P:], ps_s[half][:, i, j * P:], ACT.Exp, scale=DH ** -0.5 / QSCALE)
                        ins.then_inc(s_ex, 1)
                    if q >= 1 and QUADS[q - 1][0] != c:
                        osb_out(act, h, q - 1, more)
                osb_out(act, h, NQ - 1, more)

        @block.tensor
        def _(pe):
            t_ = nc.tensor
            pe.wait_ge(s_const, 16 * NLOADS)

            def slot_free(use):
                pe.wait_ge(s_mr, use - MRING + 1)

            def unit(b, u, slot):
                i, j = MUNITS[u]
                width = min(CH, (i + 1) * P - j * CH)
                diagonal = j == i // TPC
                ins = t_.matmul(ps_m[slot][:, 0:width], qs[b][0:SROWS, i * P:(i + 1) * P],
                                ks[b][0:SROWS, j * CH:j * CH + width], start=True, stop=not diagonal)
                if diagonal:
                    ins = t_.matmul(ps_m[slot][:, width - P:width], ident16[:, :], mask_q[:, :], start=False, stop=True)
                ins.then_inc(s_mm, 1)

            def turn(h, slot):
                pe.wait_ge(s_np, h + 1)
                t_.matmul(ps_m[slot][0:PARTS * NT, 0:P], nparts[:, :, :].rearrange("p r t -> p (r t)"), ident16[:, :],
                          start=True, stop=True).then_inc(s_mm, 1)

            def scores(b, q, half):
                c, g = QUADS[q]
                for i in range(2):
                    j = 2 * half + i
                    kb = TPC * g + j
                    off = j * P if g == c and c > 0 else 0
                    diagonal = g == c
                    ins = t_.matmul(ps_s[half][:, i, off:], ks[b][0:SROWS + PARTS, kb * P:(kb + 1) * P],
                                    qs[b][0:SROWS + PARTS, c * CH + off:(c + 1) * CH], start=True, stop=not diagonal)
                    if diagonal:
                        lo = 3 * P - j * P + off
                        wide = CH if c == 0 else P
                        ins = t_.matmul(ps_s[half][:, i, off:off + wide], ident16[:, :], mask_k[:, lo:lo + wide],
                                        start=False, stop=True)
                ins.then_inc(s_st, 1)

            def product(h, b, q):
                c, g = QUADS[q]
                if g == 0:
                    pe.wait_ge(s_osb, NCH * h + c)
                pe.wait_ge(s_ex, 2 * NQ * h + 2 * q + 2)
                for j in range(TPC):
                    off = j * P if g == c and c > 0 else 0
                    ins = t_.matmul(ps_o[j * VW:(j + 1) * VW, off:], vs[b][:, TPC * g + j, :],
                                    ex[q % len(ex)][:, j, off:], start=(g == 0), stop=(g == c))
                ins.then_inc(s_pv, 1)

            def folded(h, c, slot):
                pe.wait_ge(s_osb, NCH * h + c + 1)
                for t in range(TPC):
                    ins = t_.matmul(ps_m[slot][:, t * (DH + 1):(t + 1) * (DH + 1)], osb[:, c % 2, t * P:(t + 1) * P],
                                    fold[:, :], start=True, stop=True)
                ins.then_inc(s_mm, 1)

            pe.wait_ge(s_load, 16 * NLOAD)
            pe.wait_ge(s_ones, 1)
            for u in range(NM):
                if u >= MRING:
                    slot_free(u)
                unit(0, u, u % MRING)
            slot_free(NM)
            turn(0, NM % MRING)
            for h, b, more in heads(pe):
                pe.wait_ge(s_nload, 16 * PARTS * (h + 1))
                pe.wait_ge(s_vs, h + 1)
                k = 0
                for what, n in plan(more):
                    if what == "scores":
                        q, half = n
                        pe.wait_ge(s_ex, 2 * NQ * h + (2 * q + half - 1 if q else 0))
                        scores(b, q, half)
                        continue
                    if what == "product":
                        product(h, b, n)
                        continue
                    slot = (FIRST + (0 if more else NUSE) + k) % MRING
                    if what == "unit" and n == 0:
                        pe.wait_ge(s_load, 16 * NLOAD * (h + 2))
                    slot_free(FIRST + h * NUSE + k)
                    if what == "unit":
                        unit(1 - b, n, slot)
                    elif what == "turn":
                        turn(h + 1, slot)
                    else:
                        folded(h, n, slot)
                    k += 1

        @block.vector
        def _(dve):
            v = nc.vector

            def unit_max(st, use, u, slot):
                i, j = MUNITS[u]
                width = min(CH, (i + 1) * P - j * CH)
                dve.wait_ge(s_mm, use + 1)
                v.tensor_reduce(maxes[:, u:u + 1], ps_m[slot][:, 0:width], AX.X, ALU.max).then_inc(s_mr, 1)
                c = i // TPC
                if i % TPC == TPC - 1 and j == c:
                    dve.wait_ge(s_mr, use + 1)
                    st.step(v.tensor_reduce(nmax[:, TPC * c:TPC * (c + 1)],
                                            maxes[:, u + 1 - TPC * (c + 1):u + 1].rearrange("p (t j) -> p t j", j=c + 1),
                                            AX.X, ALU.max, negate=True))
                if u == NM - 1:
                    split_maxima(st)

            def split_maxima(st):
                st.done()
                st.step(v.tensor_copy(nparts[:, 0, :], nmax[:, :]))
                st.done()
                st.step(v.tensor_tensor(nrest[:, :], nmax[:, :], nparts[:, 0, :], ALU.subtract))
                st.done()
                st.step(v.tensor_copy(nparts[:, 1, :], nrest[:, :]))
                st.done()
                v.tensor_tensor(nparts[:, 2, :], nrest[:, :], nparts[:, 1, :], ALU.subtract).then_inc(s_np, 1)

            def turned_rows(h, use, slot):
                dve.wait_ge(s_mm, use + 1)
                dve.wait_ge(s_nload, 16 * PARTS * h)
                v.tensor_copy(nrows[:, :], ps_m[slot][0:PARTS * NT, 0:P]).then_inc(s_mr, 1)

            def normalise(st, h, use, c, slot):
                dve.wait_ge(s_mm, use + 1)
                o = ps_m[slot][:, 0:TPC * (DH + 1)].rearrange("p (t d) -> p t d", d=DH + 1)
                dve.wait_ge(s_mr, use)
                st.step(v.reciprocal(rden[:, :], o[:, :, DH]))
                st.done()
                v.tensor_tensor(att[:, TPC * c:TPC * (c + 1), bass.ds(h * DH, DH)], o[:, :, 0:DH],
                                rden[:, :].rearrange("p (t a) -> p t a", a=1).to_broadcast([P, TPC, DH]),
                                ALU.mult).then_inc(s_mr, 1)

            for b in range(2):
                ins = v.memset(ks[b][SROWS:SROWS + PARTS, :], 1.0)
            ins.then_inc(s_ones, 1)
            st = Steps(dve, s_dve)
            for u in range(NM):
                unit_max(st, u, u, u % MRING)
            assert st.count == MAX_STEPS
            turned_rows(0, NM, NM % MRING)
            for h, b, more in heads(dve):
                st = Steps(dve, s_dve, MAX_STEPS + h * (MAX_STEPS + NCH))
                for k, (what, n) in enumerate(uses(more)):
                    use = FIRST + h * NUSE + k
                    slot = (FIRST + (0 if more else NUSE) + k) % MRING
                    if what == "unit":
                        unit_max(st, use, n, slot)
                    elif what == "turn":
                        turned_rows(h + 1, use, slot)
                    else:
                        normalise(st, h, use, n, slot)
                assert st.count == (MAX_STEPS if more else 0) + NCH


class Norm:

    def __init__(self, nc, sb, sem, name):
        self.v = nc.vector
        self.stats = sb(f"{name}_stats", [P, TPC, 6])
        self.mv = sb(f"{name}_mv", [P, TPC, 2])
        self.rstd = sb(f"{name}_rstd", [P, TPC])
        self.spare = sb(f"{name}_spare", [P, 1])
        self.veps = sb(f"{name}_veps", [P, TPC])
        self.eps = sb(f"{name}_eps", [P, TPC])
        self.power = sb(f"{name}_power", [P, TPC])
        self.s_var, self.s_veps, self.s_rstd = sem(f"{name}_var"), sem(f"{name}_veps"), sem(f"{name}_rstd")

    def constants(self):
        self.v.memset(self.eps[:, :], EPS)
        return self.v.memset(self.power[:, :], -0.5)

    def rows(self, dve, st, nth, src, out, out_sem=None):
        for t in range(TPC):
            ins = self.v.bn_stats(self.stats[:, t, :], src[:, t, :])
        st.step(ins)
        st.done()
        st.step(self.v.memset(self.spare[:, :], 0.0))
        for t in range(TPC):
            ins = self.v.bn_aggr(self.mv[:, t, :], self.stats[:, t, :])
        ins.then_inc(self.s_var, 1)
        dve.wait_ge(self.s_rstd, nth + 1)
        for t in range(TPC):
            ins = self.v.tensor_scalar(out[:, t, :], src[:, t, :], self.mv[:, t, 0:1], self.rstd[:, t:t + 1],
                                       ALU.subtract, ALU.mult)
        if out_sem is None:
            st.step(ins)
            st.done()
        else:
            ins.then_inc(out_sem, 1)

    def root(self, nc, pool, nth):
        pool.wait_ge(self.s_var, nth + 1)
        nc.gpsimd.tensor_tensor(self.veps[:, :], self.mv[:, :, 1], self.eps[:, :], ALU.add).then_inc(self.s_veps, 1)
        pool.wait_ge(self.s_veps, nth + 1)
        nc.gpsimd.tensor_tensor(self.rstd[:, :], self.veps[:, :], self.power[:, :], ALU.pow).then_inc(self.s_rstd, 1)


def mlp_phase(nc, a, keep):
    NORMS = 3
    NORM_STEPS = 2
    STEPS = 20
    with ExitStack() as ctx:
        def sb(name, shape, dt=F32):
            return ctx.enter_context(nc.sbuf_tensor(name, shape, dt))

        def psum(name, shape):
            return ctx.enter_context(nc.psum_tensor(name, shape, F32))

        def sem(name):
            return ctx.enter_context(nc.semaphore(name))

        out_w = sb("out_w", [P, KT, D])
        w1 = sb("w1", [P, KT, FF])
        w2 = sb("w2", [P, FT, D])
        rw = sb("rw", [P, KT, NE])
        g2 = sb("g2", [P, KT])
        b2 = sb("b2", [P, KT])
        bias1 = sb("bias1", [P, FT])
        out_b = sb("out_b", [P, D])
        bias2 = sb("bias2", [P, D])
        score_b = sb("score_b", [P, NE])
        experts = sb("experts", [P, NE])
        atts = sb("atts", [P, TPC, D])
        x0c = sb("x0c", [P, TPC, D])
        xc = sb("xc", [P, TPC, D])
        x1 = sb("x1", [P, TPC, D])
        wide = sb("wide", [P, TPC, D])
        wide_in = sb("wide_in", [P, TPC, D])
        turned = sb("turned", [P, KT, CH])
        turned_in = sb("turned_in", [P, KT, CH])
        hid = sb("hid", [P, FT, CH])
        lg = sb("lg", [P, TPC, NE])
        rwt = sb("rwt", [P, TPC, NE])
        cor = sb("cor", [P, TPC, NE])
        small = sb("small", [P, TPC])
        top = sb("top", [P, TPC, 8])
        topi = sb("topi", [P, TPC, 8], U32)
        topf = sb("topf", [P, TPC, 8])
        hit = sb("hit", [P, TPC, NE, TOPK])
        ones = sb("ones", [P, 1])
        norm = Norm(nc, sb, sem, "p4")

        ps_t = psum("ps_t", [P, KT, CH])
        ps_y = psum("ps_y", [P, TPC, D])
        ps_h = psum("ps_h", [P, 2, CH])
        ps_r = psum("ps_r", [P, CH])
        ps_c = psum("ps_c", [P, CH])

        s_const = sem("p4_const")
        s_const2 = sem("p4_const2")
        s_in = sem("p4_in")
        s_xin = sem("p4_xin")
        s_dve = sem("p4_dve")
        s_t1, s_t2, s_t3 = sem("p4_t1"), sem("p4_t2"), sem("p4_t3")
        s_c1, s_c2, s_c3 = sem("p4_c1"), sem("p4_c2"), sem("p4_c3")
        s_y1, s_y2 = sem("p4_y1"), sem("p4_y2")
        s_x0b = sem("p4_x0b")
        s_x1 = sem("p4_x1")
        s_ln2 = sem("p4_ln2")
        s_x1b = sem("p4_x1b")
        s_h = sem("p4_h")
        s_gelu = sem("p4_gelu")
        s_mlp = sem("p4_mlp")
        s_nm = sem("p4_nm")
        s_x2 = sem("p4_x2")
        s_x2out = sem("p4_x2out")
        s_x3 = sem("p4_x3")
        s_hi = sem("p4_hi")
        s_lo = sem("p4_lo")
        s_lg = sem("p4_lg")
        s_lmax = sem("p4_lmax")
        s_lexp = sem("p4_lexp")
        s_hit = sem("p4_hit")
        s_cnt = sem("p4_cnt")
        s_cntout = sem("p4_cntout")
        NLOADS = 5
        s_late = sem("p4_late")
        NLATE = 6

        x_dram = a["x"].rearrange("a (c t p) d -> c (a p) t d", t=TPC, p=P)
        x0_dram = a["x0"].rearrange("(c t p) d -> c p t d", t=TPC, p=P)
        x2_dram = a["x2"].rearrange("(c t p) d -> c p t d", t=TPC, p=P)
        x3h, x3l, comb = keep["x3h"], keep["x3l"], keep["comb"]
        ident = keep["ident"]
        block = ctx.enter_context(nc.Block())

        def row_of(x):
            return x[:, :].rearrange("p (a d) -> p a d", a=1).to_broadcast([P, TPC, D])

        @block.sync
        def _(sp):

            def load(c):
                sp.dma_start(atts[:, :, :], keep["att"][:, bass.ds(c * TPC, TPC), :]).then_inc(s_in, 16)
                sp.dma_start(x0c[:, :, :], x0_dram[bass.ds(c, 1)].rearrange("a p t d -> p (a t) d")).then_inc(s_in, 16)

            load(0)
            for to, src in ((out_w, by_part(a["out_w"])), (out_b, a["out_b"]), (g2, a["ln2_g"]), (b2, a["ln2_b"]),
                            (bias2, a["b2"])):
                sp.dma_start(to[:], src).then_inc(s_const, 16)
            for to, src in ((w1, by_part(a["w1"])), (w2, by_part(a["w2"])), (rw, by_part(a["router_w"])), (bias1, a["b1"]),
                            (score_b, a["score_bias"]), (experts, a["experts"])):
                sp.dma_start(to[:], src).then_inc(s_late, 16)
            with sp.Fori(1, NCH) as c:
                sp.wait_ge(s_x1, c)
                load(c)

        @block.gpsimd
        def _(pool):
            g = nc.gpsimd
            pool.dma_start(xc[:, :, :], x_dram[0]).then_inc(s_xin, 16)
            pool.wait_ge(s_const, 16 * NLOADS)
            pool.wait_ge(s_const2, 1)

            def first_bias(c):
                pool.wait_ge(s_in, 32 * (c + 1))
                g.tensor_tensor(x0c[:, :, :], x0c[:, :, :], row_of(out_b), ALU.add).then_inc(s_x0b, 1)

            def second_bias(c):
                pool.wait_ge(s_ln2, c + 1)
                g.tensor_tensor(x1[:, :, :], x1[:, :, :], row_of(bias2), ALU.add).then_inc(s_x1b, 1)

            def residual(c):
                pool.wait_ge(s_nm, c + 1)
                pool.wait_ge(s_xin, 16 * (c + 1))
                g.tensor_tensor(xc[:, :, :], xc[:, :, :], wide[:, :, :], ALU.add).then_inc(s_x2, 1)
                pool.wait_ge(s_x2, c + 1)
                pool.dma_start(x2_dram[bass.ds(c, 1)].rearrange("a p t d -> p (a t) d"), xc[:, :, :]).then_inc(s_x2out, 16)

            def low(c):
                pool.wait_ge(s_hi, c + 1)
                g.tensor_tensor(x3l[:, :, bass.ds(c * CH, CH)], turned[:, :, :],
                                x3h[:, :, bass.ds(c * CH, CH)].bitcast(F32), ALU.subtract).then_inc(s_lo, 1)

            first_bias(0)
            norm.root(nc, pool, 0)
            second_bias(0)
            with pool.Fori(0, NCH - 1) as c:
                first_bias(c + 1)
                norm.root(nc, pool, NORMS * c + 1)
                residual(c)
                norm.root(nc, pool, NORMS * c + 2)
                norm.root(nc, pool, NORMS * c + 3)
                second_bias(c + 1)
                low(c)
                pool.wait_ge(s_x2out, 16 * (c + 1))
                pool.wait_ge(s_x3, c + 1)
                pool.dma_start(xc[:, :, :], x_dram[bass.ds(c + 1, 1)].rearrange("a p t d -> p (a t) d")).then_inc(s_xin, 16)
            norm.root(nc, pool, NORMS * (NCH - 1) + 1)
            residual(NCH - 1)
            norm.root(nc, pool, NORMS * (NCH - 1) + 2)
            low(NCH - 1)
            pool.wait_ge(s_x2out, 16 * NCH)

        @block.scalar
        def _(act):
            s = nc.scalar
            act.wait_ge(s_const, 16 * NLOADS)

            def copy_attention(c):
                act.wait_ge(s_t1, c + 1)
                s.activation(turned_in[:, :, :], ps_t[:, :, :], ACT.Copy).then_inc(s_c1, 1)

            def copy_norm(c):
                act.wait_ge(s_y1, c + 1)
                act.wait_ge(s_t2, c + 1)
                for m in range(KT):
                    ins = s.activation(turned_in[:, m, :], ps_t[:, m, :], ACT.Identity, bias=b2[:, m:m + 1],
                                       scale=g2[:, m:m + 1])
                ins.then_inc(s_c2, 1)

            def hidden(c):
                act.wait_ge(s_y2, c)
                for f in range(FT):
                    act.wait_ge(s_h, FT * c + f + 1)
                    s.activation(hid[:, f, :], ps_h[:, f % 2, :], ACT.Gelu, bias=bias1[:, f:f + 1]).then_inc(s_gelu, 1)

            def copy_x3(c):
                act.wait_ge(s_lo, c)
                act.wait_ge(s_lg, c)
                act.wait_ge(s_t3, c + 1)
                s.activation(turned[:, :, :], ps_t[:, :, :], ACT.Copy).then_inc(s_c3, 1)
                s.activation(x3h[:, :, bass.ds(c * CH, CH)], ps_t[:, :, :], ACT.Copy).then_inc(s_hi, 1)

            def exponentials(c):
                act.wait_ge(s_lmax, c + 1)
                s.activation(rwt[:, :, :], lg[:, :, :], ACT.Exp).then_inc(s_lexp, 1)

            copy_attention(0)
            copy_norm(0)
            act.wait_ge(s_late, 16 * NLATE)
            hidden(0)
            with act.Fori(0, NCH - 1) as c:
                copy_attention(c + 1)
                copy_norm(c + 1)
                hidden(c + 1)
                copy_x3(c)
                exponentials(c)
            copy_x3(NCH - 1)
            exponentials(NCH - 1)

        @block.tensor
        def _(pe):
            t_ = nc.tensor
            pe.wait_ge(s_const, 16 * NLOADS)

            def turn(src, sem):
                for t in range(TPC):
                    for m in range(KT):
                        ins = t_.transpose(ps_t[:, m, t * P:(t + 1) * P], src[:, t, m * P:(m + 1) * P], ident[:, :])
                ins.then_inc(sem, 1)

            def project(c):
                pe.wait_ge(s_in, 32 * (c + 1))
                if not isinstance(c, int) or c >= 2:
                    pe.wait_ge(s_hi, c - 1)
                turn(atts, s_t1)
                pe.wait_ge(s_mlp, c)
                pe.wait_ge(s_c1, c + 1)
                for t in range(TPC):
                    for k in range(KT):
                        ins = t_.matmul(ps_y[:, t, :], turned_in[:, k, t * P:(t + 1) * P], out_w[:, k, :],
                                        start=(k == 0), stop=(k == KT - 1))
                ins.then_inc(s_y1, 1)

            def turn_norm(c):
                pe.wait_ge(s_ln2, c + 1)
                turn(wide_in, s_t2)

            def mlp(c, between=None):
                pe.wait_ge(s_c2, c + 1)
                for f in range(FT):
                    pe.wait_ge(s_gelu, FT * c + (f - 1 if f >= 2 else 0))
                    for k in range(KT):
                        ins = t_.matmul(ps_h[:, f % 2, :], w1[:, k, f * P:(f + 1) * P], turned_in[:, k, :],
                                        start=(k == 0), stop=(k == KT - 1))
                    ins.then_inc(s_h, 1)
                if between:
                    between()
                pe.wait_ge(s_x1, c + 1)
                pe.wait_ge(s_gelu, FT * (c + 1))
                for t in range(TPC):
                    for f in range(FT):
                        ins = t_.matmul(ps_y[:, t, :], hid[:, f, t * P:(t + 1) * P], w2[:, f, :],
                                        start=(f == 0), stop=(f == FT - 1))
                ins.then_inc(s_y2, 1)

            def router(c):
                pe.wait_ge(s_x3, c + 1)
                turn(wide, s_t3)
                pe.wait_ge(s_c3, c + 1)
                pe.wait_ge(s_lmax, c)
                for t in range(TPC):
                    for k in range(KT):
                        ins = t_.matmul(ps_r[:, t * NE:(t + 1) * NE], turned[:, k, t * P:(t + 1) * P], rw[:, k, :],
                                        start=(k == 0), stop=(k == KT - 1))
                ins.then_inc(s_lg, 1)

            def count(c):
                pe.wait_ge(s_hit, c + 1)
                pe.wait_ge(s_cntout, c)
                for t in range(TPC):
                    ins = t_.matmul(ps_c[0:1, 0:NE], ones[:, :], cor[:, t, :], start=(t == 0), stop=(t == TPC - 1))
                ins.then_inc(s_cnt, 1)

            project(0)
            turn_norm(0)
            pe.wait_ge(s_late, 16 * NLATE)
            mlp(0)
            with pe.Fori(0, NCH - 1) as c:
                project(c + 1)
                turn_norm(c + 1)
                mlp(c + 1, between=lambda: router(c))
                count(c)
            router(NCH - 1)
            count(NCH - 1)

        @block.vector
        def _(dve):
            v = nc.vector
            v.memset(ones[:, :], 1.0)
            v.memset(comb[:, NE:FILLER, :], 1.0)
            v.memset(comb[:, FILLER, :], 0.0)
            norm.constants().then_inc(s_const2, 1)
            dve.wait_ge(s_const2, 1)
            dve.wait_ge(s_const, 16 * NLOADS)

            def over(x, n):
                return x.rearrange("p (t a) -> p t a", a=1).to_broadcast([P, TPC, n])

            def before_mlp(st, c, nth):
                dve.wait_ge(s_nm, c)
                dve.wait_ge(s_x0b, c + 1)
                dve.wait_ge(s_y1, c + 1)
                v.tensor_tensor(x1[:, :, :], ps_y[:, :, :], x0c[:, :, :], ALU.add).then_inc(s_x1, 1)
                dve.wait_ge(s_x1, c + 1)
                norm.rows(dve, st, nth, x1, wide_in, s_ln2)

            def after_mlp(st, c, nth):
                dve.wait_ge(s_x1b, c + 1)
                dve.wait_ge(s_y2, c + 1)
                v.tensor_tensor(x1[:, :, :], ps_y[:, :, :], x1[:, :, :], ALU.add).then_inc(s_mlp, 1)
                dve.wait_ge(s_mlp, c + 1)
                norm.rows(dve, st, nth, x1, wide, s_nm)

            def route(st, c, nth):
                def step(ins):
                    st.step(ins)
                    st.done()

                dve.wait_ge(s_x2, c + 1)
                norm.rows(dve, st, nth, xc, wide, s_x3)
                dve.wait_ge(s_lg, c + 1)
                logits = ps_r[:, 0:TPC * NE].rearrange("p (t e) -> p t e", e=NE)
                step(v.tensor_reduce(small[:, :], logits, AX.X, ALU.max))
                v.tensor_tensor(lg[:, :, :], logits, over(small[:, :], NE), ALU.subtract).then_inc(s_lmax, 1)
                dve.wait_ge(s_lexp, c + 1)
                step(v.tensor_reduce(small[:, :], rwt[:, :, :], AX.X, ALU.add))
                step(v.reciprocal(small[:, :], small[:, :]))
                step(v.tensor_tensor(rwt[:, :, :], rwt[:, :, :], over(small[:, :], NE), ALU.mult))
                step(v.tensor_tensor(cor[:, :, :], rwt[:, :, :],
                                     score_b[:, :].rearrange("p (a e) -> p a e", a=1).to_broadcast([P, TPC, NE]), ALU.add))
                v.memset(norm.spare[:, :], 0.0)
                for t in range(TPC):
                    ins = v.max(top[:, t, :], cor[:, t, :])
                step(ins)
                st.step(v.memset(norm.spare[:, :], 1.0))
                for t in range(TPC):
                    ins = v.max_index(topi[:, t, :], top[:, t, :], cor[:, t, :])
                step(ins)
                step(v.tensor_copy(topf[:, :, :], topi[:, :, :]))
                step(v.tensor_tensor(hit[:, :, :, :],
                                     experts[:, :].rearrange("p (a e k) -> p a e k", a=1, k=1).to_broadcast([P, TPC, NE, TOPK]),
                                     topf[:, :, 0:TOPK].rearrange("p t (a k) -> p t a k", a=1).to_broadcast([P, TPC, NE, TOPK]),
                                     ALU.is_equal))
                v.tensor_reduce(cor[:, :, :], hit[:, :, :, :], AX.X, ALU.add).then_inc(s_hit, 1)
                dve.wait_ge(s_hit, c + 1)
                step(v.tensor_tensor(rwt[:, :, :], rwt[:, :, :], cor[:, :, :], ALU.mult))
                step(v.tensor_reduce(small[:, :], rwt[:, :, :], AX.X, ALU.add))
                step(v.tensor_scalar(small[:, :], small[:, :], 1e-12, None, ALU.max))
                step(v.reciprocal(small[:, :], small[:, :]))
                v.tensor_tensor(comb[:, 0:NE, bass.ds(c * TPC, TPC)].rearrange("p e t -> p t e"), rwt[:, :, :],
                                over(small[:, :], NE), ALU.mult)
                dve.wait_ge(s_cnt, c + 1)
                v.tensor_copy(keep["counts"][0:1, bass.ds(c * NE, NE)], ps_c[0:1, 0:NE]).then_inc(s_cntout, 1)

            before_mlp(Steps(dve, s_dve), 0, 0)
            dve.wait_ge(s_late, 16 * NLATE)
            with dve.Fori(0, NCH - 1) as c:
                st = Steps(dve, s_dve, c * STEPS + NORM_STEPS)
                after_mlp(st, c, NORMS * c + 1)
                before_mlp(st, c + 1, NORMS * c + 2)
                route(st, c, NORMS * c + 3)
                assert st.count == STEPS, st.count
            st = Steps(dve, s_dve, (NCH - 1) * STEPS + NORM_STEPS)
            after_mlp(st, NCH - 1, NORMS * (NCH - 1) + 1)
            route(st, NCH - 1, NORMS * (NCH - 1) + 2)


def list_phase(nc, a, keep):
    with ExitStack() as ctx:
        def sb(name, shape, dt=F32):
            return ctx.enter_context(nc.sbuf_tensor(name, shape, dt))

        def sem(name):
            return ctx.enter_context(nc.semaphore(name))

        HALVES = NCH * NE // P
        one = sb("one", [P, P])
        upto = sb("upto", [P, P])
        places = sb("places", [P, NCH * NE])
        codes = sb("codes", [P, HALVES, 2])
        counts_row = sb("counts_row", [1, NCH * NE])
        chosen = sb("chosen", [P, HALVES])
        rank = sb("rank", [P, HALVES + 1])
        starts = sb("starts", [1, NCH * NE // ROUND])
        count = sb("count", [1, 1])
        at_place = sb("at_place", [P, HALVES, NCH * NE])
        psum = ctx.enter_context(nc.psum_tensor("ps_list", [P, 3, CH], F32))
        s_const = sem("l_const")
        s_one = sem("l_one")
        s_row = sem("l_row")
        s_col = sem("l_col")
        s_chosen = sem("l_chosen")
        s_rank = sem("l_rank")
        s_place = sem("l_place")
        s_list = sem("l_list")
        s_rk = sem("l_rk")
        block = ctx.enter_context(nc.Block())
        listed, more_rounds = keep["listed"], keep["more_rounds"]

        @block.sync
        def _(sp):
            for to, src in ((upto[:, :], a["upto"]), (places[:, :], a["places"]), (codes[:, :, :], a["codes"]),
                            (listed[:, :, :], a["listed"])):
                sp.dma_start(to, src).then_inc(s_const, 16)

        @block.tensor
        def _(pe):
            t_ = nc.tensor
            pe.wait_ge(s_one, 1)
            pe.wait_ge(s_row, 1)
            for h in range(HALVES):
                ins = t_.matmul(psum[:, 0, h:h + 1], counts_row[0:1, h * P:(h + 1) * P], one[0:1, 0:1], start=True, stop=True)
            ins.then_inc(s_col, 1)
            pe.wait_ge(s_chosen, 1)
            pe.wait_ge(s_const, 64)
            for h in range(HALVES):
                for k in range(h + 1):
                    ins = t_.matmul(psum[:, 1, h:h + 1], (upto if k == h else one)[:, :], chosen[:, k:k + 1],
                                    start=(k == 0), stop=(k == h))
            for k in range(HALVES):
                ins = t_.matmul(psum[:, 1, HALVES:HALVES + 1], one[:, :], chosen[:, k:k + 1], start=(k == 0),
                                stop=(k == HALVES - 1))
            ins.then_inc(s_rank, 1)
            pe.wait_ge(s_place, 1)
            for n in range(2):
                for k in range(HALVES):
                    ins = t_.matmul(psum[0:1, 2, n * NCH * NE:(n + 1) * NCH * NE], codes[:, k, n:n + 1], at_place[:, k, :],
                                    start=(k == 0), stop=(k == HALVES - 1))
            ins.then_inc(s_list, 1)

        @block.vector
        def _(dve):
            v = nc.vector
            v.memset(one[:, :], 1.0).then_inc(s_one, 1)
            v.tensor_copy(counts_row[0:1, :], keep["counts"][0:1, :]).then_inc(s_row, 1)
            dve.wait_ge(s_col, 1)
            v.tensor_scalar(chosen[:, :], psum[:, 0, 0:HALVES], 0.0, None, ALU.is_gt).then_inc(s_chosen, 1)
            dve.wait_ge(s_rank, 1)
            v.tensor_copy(rank[:, :], psum[:, 1, 0:HALVES + 1]).then_inc(s_rk, 1)
            dve.wait_ge(s_rk, 1)
            dve.wait_ge(s_chosen, 1)
            dve.wait_ge(s_const, 64)
            for h in range(HALVES):
                ins = v.tensor_scalar(at_place[:, h, :], places[:, :], rank[:, h:h + 1], chosen[:, h:h + 1],
                                      ALU.is_equal, ALU.mult)
            ins.then_inc(s_place, 1)
            v.tensor_scalar(starts[0:1, :], places[0:1, :].rearrange("a (r i) -> a r i", i=ROUND)[:, :, 0],
                            rank[0:1, HALVES:HALVES + 1], None, ALU.is_le).then_inc(s_rk, 1)
            dve.wait_ge(s_rk, 2)
            v.tensor_reduce(count[0:1, :], starts[0:1, :], AX.X, ALU.add).then_inc(s_rk, 1)
            dve.wait_ge(s_rk, 3)
            v.tensor_scalar(more_rounds[0:1, :], count[0:1, :], float(FIXED // ROUND - 1), None, ALU.add)
            dve.wait_ge(s_list, 1)
            v.tensor_scalar(listed[0:1, 0, FIXED:FIXED + NCH * NE], psum[0:1, 2, 0:NCH * NE], float(FILLER), None, ALU.add)
            v.tensor_copy(listed[0:1, 1, FIXED:FIXED + NCH * NE], psum[0:1, 2, NCH * NE:])


def expert_phase(nc, a, keep):
    GU = KT * 2 * NI
    EW = GU + D
    with ExitStack() as ctx:
        def sb(name, shape, dt=F32):
            return ctx.enter_context(nc.sbuf_tensor(name, shape, dt))

        def psum(name, shape):
            return ctx.enter_context(nc.psum_tensor(name, shape, F32))

        def sem(name):
            return ctx.enter_context(nc.semaphore(name))

        raw = [sb(f"raw{i}", [P, EW]) for i in range(ROUND)]
        wh = [sb(f"wh{i}", [P, EW], F32R) for i in range(ROUND)]
        wl = [sb(f"wl{i}", [P, EW], F32R) for i in range(ROUND)]
        sg = [sb(f"sg{i}", [P, CH]) for i in range(2)]
        hh = [sb(f"hh{i}", [P, CH]) for i in range(2)]
        hhi = [sb(f"hhi{i}", [P, CH], F32R) for i in range(2)]
        hlo = [sb(f"hlo{i}", [P, CH], F32R) for i in range(2)]
        y, x3h, x3l, comb = keep["y"], keep["x3h"], keep["x3l"], keep["comb"]
        listed = keep["listed"]

        ps_g = [psum(f"ps_g{i}", [P, CH]) for i in range(2)]
        ps_u = [psum(f"ps_u{i}", [P, CH]) for i in range(2)]
        ps_y = [psum(f"ps_yy{i}", [P, TPC, D]) for i in range(2)]

        s_zero = sem("p5_zero")
        s_raw = [sem(f"p5_raw{i}") for i in range(ROUND)]
        s_wh = sem("p5_wh")
        s_wl = sem("p5_wl")
        s_gu = sem("p5_gu")
        s_silu = sem("p5_silu")
        s_hh = sem("p5_hh")
        s_hhi = sem("p5_hhi")
        s_hlo = sem("p5_hlo")
        s_dn = sem("p5_dn")
        s_yy = sem("p5_yy")
        AHEAD = 2
        block = ctx.enter_context(nc.Block())

        def loaded(engine, which, u, limit):
            return engine.value_load(listed[0:1, which, bass.ds(u, 1)], min_val=0, max_val=limit)

        def rounds(engine, step, finish):
            for i in range(ROUND):
                step(i, i)
            after_first = engine.value_load(keep["more_rounds"][0:1, 0:1], min_val=0, max_val=ROUNDS - 1)
            with engine.Fori(0, SPANS) as span:
                with engine.If(span * SPAN < after_first):
                    with engine.Fori(0, SPAN) as one:
                        r = span * SPAN + one + 1
                        with engine.If(r <= after_first):
                            for i in range(ROUND):
                                step(r * ROUND + i, i)
            finish(after_first * ROUND + ROUND)

        def wait_past(engine, sem, u, back):
            if not isinstance(u, int):
                engine.wait_ge(sem, u + (1 - back))
            elif u >= back:
                engine.wait_ge(sem, u + 1 - back)

        @block.sync
        def _(sp):
            def load(u, i):
                wait_past(sp, s_wl, u, ROUND)
                e = loaded(sp, 0, u, FILLER)
                sp.dma_start(raw[i][:, :], a["experts_w"][bass.ds(e, 1)].rearrange("a p n -> p (a n)")).then_inc(s_raw[i], 16)

            def finish(n):
                for i in range(AHEAD):
                    sp.wait_ge(s_wl, n + i - ROUND + 1)
                    sp.dma_start(raw[i][:, :], a["experts_w"][FILLER]).then_inc(s_raw[i], 16)

            rounds(sp, load, finish)

        @block.scalar
        def _(act):
            s = nc.scalar

            def high(u, i):
                act.wait_ge(s_raw[i], (16 // ROUND) * (u - i) + 16)
                wait_past(act, s_dn, u, ROUND)
                s.activation(wh[i][:, :], raw[i][:, :], ACT.Copy).then_inc(s_wh, 1)

            def step(u, i):
                b = i % 2
                act.wait_ge(s_gu, u + 1)
                wait_past(act, s_hh, u, 2)
                s.activation(sg[b][:, :], ps_g[b][:, :], ACT.Silu).then_inc(s_silu, 1)
                act.wait_ge(s_hh, u + 1)
                wait_past(act, s_dn, u, 2)
                s.activation(hhi[b][:, :], hh[b][:, :], ACT.Copy).then_inc(s_hhi, 1)
                high(u + AHEAD, (i + AHEAD) % ROUND)

            for i in range(AHEAD):
                high(i, i)
            rounds(act, step, lambda n: None)

        @block.gpsimd
        def _(pool):
            g = nc.gpsimd

            def low(u, i):
                pool.wait_ge(s_wh, u + 1)
                g.tensor_tensor(wl[i][:, :], raw[i][:, :], wh[i][:, :].bitcast(F32), ALU.subtract).then_inc(s_wl, 1)

            def step(u, i):
                b = i % 2
                pool.wait_ge(s_hhi, u + 1)
                g.tensor_tensor(hlo[b][:, :], hh[b][:, :], hhi[b][:, :].bitcast(F32), ALU.subtract).then_inc(s_hlo, 1)
                low(u + AHEAD, (i + AHEAD) % ROUND)

            for i in range(AHEAD):
                low(i, i)
            rounds(pool, step, lambda n: None)

        @block.tensor
        def _(pe):
            t_ = nc.tensor

            def three(out, l, r, start, stop):
                for n, (x, w) in enumerate(((0, 0), (0, 1), (1, 0))):
                    ins = t_.matmul(out, l[x], r[w], start=start and n == 0, stop=stop and n == 2, skip_group_check=True)
                return ins

            def down(u, i):
                b = i % 2
                pe.wait_ge(s_hlo, u + 1)
                wait_past(pe, s_yy, u, 2)
                w = slice(GU, GU + D)
                for t in range(TPC):
                    tk = slice(t * P, (t + 1) * P)
                    ins = three(ps_y[b][:, t, :], (hhi[b][:, tk], hlo[b][:, tk]), (wh[i][:, w], wl[i][:, w]),
                                t % 2 == 0, True)
                ins.then_inc(s_dn, 1)

            def step(u, i):
                b = i % 2
                c = loaded(pe, 1, u, NCH - 1)
                tok = bass.ds(c * CH, CH)
                pe.wait_ge(s_wl, u + 1)
                wait_past(pe, s_hh, u, 2)
                for n, to in enumerate((ps_g[b], ps_u[b])):
                    for k in range(KT):
                        lo = (k * 2 + n) * NI
                        ins = three(to[:, :], (wh[i][:, lo:lo + NI], wl[i][:, lo:lo + NI]), (x3h[:, k, tok], x3l[:, k, tok]),
                                    k == 0, k == KT - 1)
                ins.then_inc(s_gu, 1)
                if not (isinstance(u, int) and u == 0):
                    down(u - 1, (i - 1) % ROUND)

            rounds(pe, step, lambda n: down(n - 1, ROUND - 1))

        @block.vector
        def _(dve):
            v = nc.vector
            weights = comb[:, :, :].rearrange("p e n -> p (e n)")
            v.memset(y[:, :, :], 0.0).then_inc(s_zero, 1)

            def add_up(u, i):
                b = i % 2
                e = loaded(dve, 0, u, FILLER)
                c = loaded(dve, 1, u, NCH - 1)
                dve.wait_ge(s_yy, u)
                dve.wait_ge(s_dn, u + 1)
                for t in range(TPC):
                    row = y[:, bass.ds(c * TPC + t, 1), :].rearrange("p a d -> p (a d)")
                    ins = v.scalar_tensor_tensor(out=row, in0=ps_y[b][:, t, :], scalar=weights[:, bass.ds(e * NT + c * TPC + t, 1)],
                                                 in1=row, op0=ALU.mult, op1=ALU.add)
                ins.then_inc(s_yy, 1)

            def step(u, i):
                b = i % 2
                dve.wait_ge(s_silu, u + 1)
                wait_past(dve, s_hlo, u, 2)
                v.tensor_tensor(hh[b][:, :], ps_u[b][:, :], sg[b][:, :], ALU.mult).then_inc(s_hh, 1)
                if not (isinstance(u, int) and u == 0):
                    add_up(u - 1, (i - 1) % ROUND)

            dve.wait_ge(s_zero, 1)
            rounds(dve, step, lambda n: add_up(n - 1, ROUND - 1))


def output_phase(nc, a, keep):
    STEPS = 2
    with ExitStack() as ctx:
        def sb(name, shape, dt=F32):
            return ctx.enter_context(nc.sbuf_tensor(name, shape, dt))

        def sem(name):
            return ctx.enter_context(nc.semaphore(name))

        y = keep["y"]
        x2 = sb("x2", [P, 2, TPC, D])
        yn = sb("yn", [P, 2, TPC, D])
        res = sb("res", [P, 2, TPC, D])
        norm = Norm(nc, sb, sem, "p6")
        s_const = sem("p6_const")
        s_in = sem("p6_in")
        s_dve = sem("p6_dve")
        s_yn = sem("p6_yn")
        s_res = sem("p6_res")
        s_out = sem("p6_out")
        x2_dram = a["x2"].rearrange("(c t p) d -> c p t d", t=TPC, p=P)
        out_dram = a["out"].rearrange("a (c t p) d -> c (a p) t d", t=TPC, p=P)
        block = ctx.enter_context(nc.Block())

        def chunks(engine):
            with engine.Fori(0, NCH // 2) as pair:
                for b in range(2):
                    yield pair * 2 + b, b

        @block.sync
        def _(sp):
            for c, b in chunks(sp):
                sp.wait_ge(s_res, c)
                sp.dma_start(x2[:, b, :, :], x2_dram[bass.ds(c, 1)].rearrange("a p t d -> p (a t) d")).then_inc(s_in, 16)

        @block.scalar
        def _(act):
            for c, b in chunks(act):
                act.wait_ge(s_res, c + 1)
                act.dma_start(out_dram[bass.ds(c, 1)].rearrange("a p t d -> p (a t) d"), res[:, b, :, :]).then_inc(s_out, 16)
            act.wait_ge(s_out, 16 * NCH)

        @block.gpsimd
        def _(pool):
            pool.wait_ge(s_const, 1)
            for c, b in chunks(pool):
                norm.root(nc, pool, c)
                pool.wait_ge(s_in, 16 * (c + 1))
                pool.wait_ge(s_out, 16 * c)
                pool.wait_ge(s_yn, c + 1)
                nc.gpsimd.tensor_tensor(res[:, b, :, :], yn[:, b, :, :], x2[:, b, :, :], ALU.add).then_inc(s_res, 1)

        @block.vector
        def _(dve):
            norm.constants().then_inc(s_const, 1)
            dve.wait_ge(s_const, 1)
            for c, b in chunks(dve):
                st = Steps(dve, s_dve, c * STEPS)
                dve.wait_ge(s_res, c)
                norm.rows(dve, st, c, y[:, bass.ds(c * TPC, TPC), :], yn[:, b], s_yn)
                assert st.count == STEPS


def lay_out(inputs):
    import numpy as np

    bf16 = mybir.dt.np(BF16)

    def arr(name):
        return np.ascontiguousarray(inputs[name])

    def cols(x):
        return np.ascontiguousarray(x.reshape(-1, P).T)

    def rows(x):
        return np.ascontiguousarray(np.broadcast_to(x.reshape(1, -1), (P, x.size)))

    half = DH // 2
    freqs = np.exp(-np.arange(half, dtype=np.float32) * np.float32(np.log(10000.0) / half)).astype(np.float32)
    theta = np.arange(T, dtype=np.float32)[:, None] * freqs[None, :]
    cos, sin = np.cos(theta), np.sin(theta)
    shared = np.stack([np.concatenate([arr("L0_ffn_shared_gate_w")[i * NI:(i + 1) * NI],
                                       arr("L0_ffn_shared_up_w")[i * NI:(i + 1) * NI]]) for i in range(2)])
    unit = np.arange(NCH * NE).reshape(-1, P).T
    out = {
        "x": arr("L0_attn_x"), "wq": arr("L0_attn_Wq"), "wk": arr("L0_attn_Wk"), "wv": arr("L0_attn_Wv"),
        "gate_w": arr("L0_attn_gate_w"), "p_w": arr("L0_attn_p_w"), "clock_w": arr("L0_attn_clock_w"),
        "out_w": arr("L0_attn_out_w"), "w1": arr("L0_attn_mlp_w1"), "w2": arr("L0_attn_mlp_w2"),
        "gate_b": cols(arr("L0_attn_gate_b")), "p_b": cols(arr("L0_attn_p_b")),
        "ln1_g": cols(arr("L0_attn_ln1_g")), "ln1_b": cols(arr("L0_attn_ln1_b")),
        "ln2_g": cols(arr("L0_attn_ln2_g")), "ln2_b": cols(arr("L0_attn_ln2_b")),
        "b1": cols(arr("L0_attn_mlp_b1")),
        "clock_b": rows(arr("L0_attn_clock_b")), "out_b": rows(arr("L0_attn_out_b")), "b2": rows(arr("L0_attn_mlp_b2")),
        "score_bias": rows(arr("L0_ffn_e_score_bias")),
        "router_w": np.ascontiguousarray(arr("L0_ffn_router_weight").T),
        "experts_w": np.concatenate([
            np.concatenate([arr("L0_ffn_gate_up_proj").transpose(0, 2, 1).reshape(NE, KT, P, 2 * NI).transpose(0, 2, 1, 3)
                            .reshape(NE, P, -1), arr("L0_ffn_down_proj").transpose(0, 2, 1)], axis=2),
            np.concatenate([shared.transpose(0, 2, 1).reshape(2, KT, P, 2 * NI).transpose(0, 2, 1, 3).reshape(2, P, -1),
                            arr("L0_ffn_shared_down_w").T.reshape(2, NI, D)], axis=2),
            np.zeros((1, P, (KT * 2 + 2) * NI), np.float32)]),
        "rot_c": np.repeat(cos, 2, axis=1).astype(np.float32),
        "rot_s": np.stack([-sin, sin], -1).reshape(T, DH).astype(np.float32),
        "experts": rows(np.arange(NE, dtype=np.float32)),
        "listed": np.stack([np.r_[NE + np.arange(FIXED) % 2, np.full(ROUND * ROUNDS - FIXED, FILLER)],
                            np.r_[np.arange(FIXED) // 2, np.zeros(ROUND * ROUNDS - FIXED)]])[None].astype(np.uint32),
        "upto": np.triu(np.ones((P, P), np.float32)),
        "places": rows(np.arange(1, NCH * NE + 1, dtype=np.float32)),
        "codes": np.ascontiguousarray(np.stack([unit % NE - FILLER, unit // NE], -1).astype(np.float32)),
        "eye": np.eye(P, dtype=np.float32),
        "eye16": np.eye(P).astype(bf16),
        "mask_q": np.where(np.arange(P)[None, :] > np.arange(P)[:, None], BIG, 0.0).astype(bf16),
        "mask_k": np.where(np.arange(CH + 3 * P)[None, :] - 3 * P < np.arange(P)[:, None], BIG, 0.0).astype(bf16),
        "fold": (np.arange(P)[:, None] % (2 * DH) == np.arange(DH + 1)[None, :]).astype(np.float32),
    }
    return out


def build_kernel(nc, a):
    with ExitStack() as ctx:
        a["x0"] = nc.dram_tensor("x0_scratch", [T, D], F32).ap()
        a["qkt"] = nc.dram_tensor("qkt_scratch", [2 * D, T], F32).ap()
        a["parts"] = nc.dram_tensor("parts_scratch", [2, PARTS, D, T], BF16).ap()
        a["x2"] = nc.dram_tensor("x2_scratch", [T, D], F32).ap()

        region = T * KT * 4
        top = nc.sbuf_usable_end // 256 * 256

        def at(name, shape, dt, start):
            return nc.alloc_sbuf_tensor_at(name, shape, dt, offset=top - start)

        keep = {
            "att": at("att", [P, NT, D], F32, region),
            "v": at("v_all", [P, NT, D], F32, 2 * region),
            "pt": at("pt", [P, KT, T], F32, 3 * region),
            "gt": at("gt", [P, KT, T], F32, 4 * region),
            "p1_wide": at("p1_wide", [P, 4, TPC, 2 * D], F32, region),
            "comb": at("comb", [P, NE + 3, NT], F32, 2 * region),
            "counts": at("counts", [1, NCH * NE], F32, 2 * region - (NE + 3) * NT * 4),
            "listed": at("unit_list", [1, 2, ROUND * ROUNDS], U32, region + 8192),
            "more_rounds": at("more_rounds", [1, 1], U32, region + 4096),
            "x3h": at("x3h", [P, KT, T], F32R, 3 * region),
            "x3l": at("x3l", [P, KT, T], F32R, 4 * region),
            "y": at("y", [P, NT, D], F32, region),
            "ident": ctx.enter_context(nc.sbuf_tensor("ident", [P, P], F32)),
            "clk": ctx.enter_context(nc.sbuf_tensor("clk", [P, NT, H], F32)),
        }
        with nc.semaphore("k0_ident") as s_ident, nc.Block() as block:
            @block.sync
            def _(sp):
                sp.dma_start(keep["ident"][:, :], a["eye"]).then_inc(s_ident, 16)
                sp.wait_ge(s_ident, 16)
        for phase in (project_phase, stack_phase, attention_phase, mlp_phase, list_phase,
                      expert_phase, output_phase):
            phase(nc, a, keep)


def kernel(**inputs):
    import numpy as np
    import concourse.bacc as bacc
    from concourse.bass_utils import run_bass_kernel_spmd as run

    arrays = lay_out(inputs)
    nc = bacc.Bacc("TRN2", target_bir_lowering=False, num_devices=1)
    a = {name: nc.dram_tensor(f"in_{name}", x.shape, mybir.dt.from_np(x.dtype), kind="ExternalInput").ap()
         for name, x in arrays.items()}
    a["out"] = nc.dram_tensor("out", [1, T, D], F32, kind="ExternalOutput").ap()
    build_kernel(nc, a)
    r = run(nc, [{f"in_{name}": x for name, x in arrays.items()}], core_ids=[0])
    return r.results[0]["out"]
```
